# Optimizing a Trainium2 kernel written in Bass

```python
import numpy as np
import jax
import jax.numpy as jnp

def _softmax(x, axis=-1):
    return jax.nn.softmax(x, axis=axis)

def _gelu(x):
    return jax.nn.gelu(x, approximate=True)

def _silu(x):
    return jax.nn.silu(x)

def _sigmoid(x):
    return jax.nn.sigmoid(x)

def _layernorm(x, axis=-1, eps=1e-05):
    m = jnp.mean(x, axis=axis, keepdims=True)
    v = jnp.var(x, axis=axis, keepdims=True)
    return (x - m) / jnp.sqrt(v + eps)

def _scatter_add(tgt, idx, src, axis=0):
    return tgt.at[idx].add(src)

def _segment_sum(src, seg, n):
    return jax.ops.segment_sum(src, seg, n)
kernel_name = 'mk_sandwich_d1_jaxref_r4_c9ff54'

def setup_inputs(seed: int=0):
    np.random.seed(seed)
    _w = jnp.asarray

    def _L0_attn_setup():
        import jax, jax.numpy as jnp
        import numpy as np
        DIM = 256
        D_STATE = 16
        D_CONV = 4
        EXPAND = 2
        D_INNER = EXPAND * DIM
        BATCH = 4
        SEQ = 512

        def _reference_tuple_inner(x, in_proj_w, conv_w, x_proj_w, dt_proj_w, dt_proj_b, A_log, D, out_proj_w, norm_w, norm_b):
            Bsz, L, _ = x.shape
            shortcut = x
            mu = jnp.mean(x, axis=-1, keepdims=True)
            var = jnp.var(x, axis=-1, keepdims=True)
            h = (x - mu) / jnp.sqrt(var + 1e-05) * norm_w + norm_b
            h = h @ in_proj_w.T
            hp = jnp.pad(h, ((0, 0), (D_CONV - 1, 0), (0, 0)))
            h_conv = sum((hp[:, k:k + L, :] * conv_w[:, k] for k in range(D_CONV)))
            h = jax.nn.silu(h_conv)
            proj = h @ x_proj_w.T
            dt_in = proj[..., :1]
            B_param = proj[..., 1:1 + D_STATE]
            C_param = proj[..., 1 + D_STATE:]
            dt = jax.nn.softplus(dt_in @ dt_proj_w.T + dt_proj_b)
            A = -jnp.exp(A_log)

            def step(state, inp):
                dt_t, B_t, C_t, x_t = inp
                state = jnp.exp(A[None] * dt_t[:, :, None]) * state + B_t[:, None, :] * x_t[:, :, None]
                y = jnp.einsum('bnd,bd->bn', state, C_t) + D * x_t
                return (state, y)
            init = jnp.zeros((Bsz, D_INNER, D_STATE), x.dtype)
            xs = (jnp.swapaxes(dt, 0, 1), jnp.swapaxes(B_param, 0, 1), jnp.swapaxes(C_param, 0, 1), jnp.swapaxes(h, 0, 1))
            state, ys = jax.lax.scan(step, init, xs)
            y = jnp.swapaxes(ys, 0, 1)
            out = jax.nn.silu(y) @ out_proj_w.T + shortcut
            return (out, state)
        key = jax.random.key(seed)
        ks = jax.random.split(key, 9)
        n = lambda i, shape, scale=0.02: jax.random.normal(ks[i], shape, jnp.float32) * scale
        return {'x': jax.random.normal(ks[0], (BATCH, SEQ, DIM), jnp.float32), 'in_proj_w': n(1, (D_INNER, DIM)), 'conv_w': n(2, (D_INNER, D_CONV), 0.1), 'x_proj_w': n(3, (2 * D_STATE + 1, D_INNER)), 'dt_proj_w': n(4, (D_INNER, 1), 1.0), 'dt_proj_b': n(5, (D_INNER,), 0.1), 'A_log': jax.random.normal(ks[6], (D_INNER, D_STATE), jnp.float32), 'D': jnp.ones((D_INNER,), jnp.float32), 'out_proj_w': n(7, (DIM, D_INNER)), 'norm_w': jnp.ones((DIM,), jnp.float32), 'norm_b': jnp.zeros((DIM,), jnp.float32)}
    _L0_attn_in = _L0_attn_setup()

    def _L0_ffn_setup():
        import jax, jax.numpy as jnp
        import numpy as np
        H = 256
        I = 512
        E = 8
        B, S = (2, 256)

        def _swiglu(x, wg, wu, wd):
            return jax.nn.silu(x @ wg) * (x @ wu) @ wd
        key = jax.random.key(seed)
        ks = jax.random.split(key, 8)
        sc_h = 1.0 / np.sqrt(H)
        sc_i = 1.0 / np.sqrt(I)
        return {'hidden_states': jax.random.normal(ks[0], (B, S, H), jnp.float32), 'gate_w': jax.random.normal(ks[1], (H, E), jnp.float32) * sc_h, 'sh_gate': jax.random.normal(ks[2], (H, I), jnp.float32) * sc_h, 'sh_up': jax.random.normal(ks[3], (H, I), jnp.float32) * sc_h, 'sh_down': jax.random.normal(ks[4], (I, H), jnp.float32) * sc_i, 'rt_gate': jax.random.normal(ks[5], (E, H, I), jnp.float32) * sc_h, 'rt_up': jax.random.normal(ks[6], (E, H, I), jnp.float32) * sc_h, 'rt_down': jax.random.normal(ks[7], (E, I, H), jnp.float32) * sc_i}
    _L0_ffn_in = _L0_ffn_setup()
    _d = {'L0_attn_x': _L0_attn_in['x'], 'L0_attn_in_proj_w': _L0_attn_in['in_proj_w'], 'L0_attn_conv_w': _L0_attn_in['conv_w'], 'L0_attn_x_proj_w': _L0_attn_in['x_proj_w'], 'L0_attn_dt_proj_w': _L0_attn_in['dt_proj_w'], 'L0_attn_dt_proj_b': _L0_attn_in['dt_proj_b'], 'L0_attn_A_log': _L0_attn_in['A_log'], 'L0_attn_D': _L0_attn_in['D'], 'L0_attn_out_proj_w': _L0_attn_in['out_proj_w'], 'L0_attn_norm_w': _L0_attn_in['norm_w'], 'L0_attn_norm_b': _L0_attn_in['norm_b'], 'L0_ffn_gate_w': _L0_ffn_in['gate_w'], 'L0_ffn_sh_gate': _L0_ffn_in['sh_gate'], 'L0_ffn_sh_up': _L0_ffn_in['sh_up'], 'L0_ffn_sh_down': _L0_ffn_in['sh_down'], 'L0_ffn_rt_gate': _L0_ffn_in['rt_gate'], 'L0_ffn_rt_up': _L0_ffn_in['rt_up'], 'L0_ffn_rt_down': _L0_ffn_in['rt_down']}
    _x0 = _d['L0_attn_x']
    _d['L0_attn_x'] = jax.random.normal(jax.random.fold_in(jax.random.key(seed), 1), (8, 512, 256), dtype=_x0.dtype)
    del _x0
    return _d

def reference(L0_attn_x, L0_attn_in_proj_w, L0_attn_conv_w, L0_attn_x_proj_w, L0_attn_dt_proj_w, L0_attn_dt_proj_b, L0_attn_A_log, L0_attn_D, L0_attn_out_proj_w, L0_attn_norm_w, L0_attn_norm_b, L0_ffn_gate_w, L0_ffn_sh_gate, L0_ffn_sh_up, L0_ffn_sh_down, L0_ffn_rt_gate, L0_ffn_rt_up, L0_ffn_rt_down):

    def _L0_attn_ref(x, in_proj_w, conv_w, x_proj_w, dt_proj_w, dt_proj_b, A_log, D, out_proj_w, norm_w, norm_b):
        import jax, jax.numpy as jnp
        import numpy as np
        DIM = 256
        D_STATE = 16
        D_CONV = 4
        EXPAND = 2
        D_INNER = EXPAND * DIM
        BATCH = 4
        SEQ = 512

        def _reference_tuple_inner(x, in_proj_w, conv_w, x_proj_w, dt_proj_w, dt_proj_b, A_log, D, out_proj_w, norm_w, norm_b):
            Bsz, L, _ = x.shape
            shortcut = x
            mu = jnp.mean(x, axis=-1, keepdims=True)
            var = jnp.var(x, axis=-1, keepdims=True)
            h = (x - mu) / jnp.sqrt(var + 1e-05) * norm_w + norm_b
            h = h @ in_proj_w.T
            hp = jnp.pad(h, ((0, 0), (D_CONV - 1, 0), (0, 0)))
            h_conv = sum((hp[:, k:k + L, :] * conv_w[:, k] for k in range(D_CONV)))
            h = jax.nn.silu(h_conv)
            proj = h @ x_proj_w.T
            dt_in = proj[..., :1]
            B_param = proj[..., 1:1 + D_STATE]
            C_param = proj[..., 1 + D_STATE:]
            dt = jax.nn.softplus(dt_in @ dt_proj_w.T + dt_proj_b)
            A = -jnp.exp(A_log)

            def step(state, inp):
                dt_t, B_t, C_t, x_t = inp
                state = jnp.exp(A[None] * dt_t[:, :, None]) * state + B_t[:, None, :] * x_t[:, :, None]
                y = jnp.einsum('bnd,bd->bn', state, C_t) + D * x_t
                return (state, y)
            init = jnp.zeros((Bsz, D_INNER, D_STATE), x.dtype)
            xs = (jnp.swapaxes(dt, 0, 1), jnp.swapaxes(B_param, 0, 1), jnp.swapaxes(C_param, 0, 1), jnp.swapaxes(h, 0, 1))
            state, ys = jax.lax.scan(step, init, xs)
            y = jnp.swapaxes(ys, 0, 1)
            out = jax.nn.silu(y) @ out_proj_w.T + shortcut
            return (out, state)
        return _reference_tuple_inner(x, in_proj_w, conv_w, x_proj_w, dt_proj_w, dt_proj_b, A_log, D, out_proj_w, norm_w, norm_b)[0]

    def _L0_ffn_ref(hidden_states, gate_w, sh_gate, sh_up, sh_down, rt_gate, rt_up, rt_down):
        import jax, jax.numpy as jnp
        import numpy as np
        H = 256
        I = 512
        E = 8
        B, S = (2, 256)

        def _swiglu(x, wg, wu, wd):
            return jax.nn.silu(x @ wg) * (x @ wu) @ wd
        b, s, h = hidden_states.shape
        x = hidden_states.reshape(-1, h)
        logits = x @ gate_w
        top_val = jnp.max(logits, axis=-1, keepdims=True)
        top_id = jnp.argmax(logits, axis=-1)
        score = jax.nn.sigmoid(top_val)
        xs = x * score
        g = jnp.einsum('th,ehi->eti', xs, rt_gate)
        u = jnp.einsum('th,ehi->eti', xs, rt_up)
        act = jax.nn.silu(g) * u
        y = jnp.einsum('eti,eih->eth', act, rt_down)
        onehot = jax.nn.one_hot(top_id, E, dtype=x.dtype)
        routed = jnp.einsum('eth,te->th', y, onehot)
        shared = _swiglu(x, sh_gate, sh_up, sh_down)
        return (shared + routed).reshape(b, s, h)
    x = L0_attn_x
    x = x + _layernorm(_L0_attn_ref(_layernorm(x, axis=-1), L0_attn_in_proj_w, L0_attn_conv_w, L0_attn_x_proj_w, L0_attn_dt_proj_w, L0_attn_dt_proj_b, L0_attn_A_log, L0_attn_D, L0_attn_out_proj_w, L0_attn_norm_w, L0_attn_norm_b), axis=-1)
    x = x + _layernorm(_L0_ffn_ref(_layernorm(x, axis=-1), L0_ffn_gate_w, L0_ffn_sh_gate, L0_ffn_sh_up, L0_ffn_sh_down, L0_ffn_rt_gate, L0_ffn_rt_up, L0_ffn_rt_down), axis=-1)
    return x

_drawn_inputs = setup_inputs


def setup_inputs(seed=0):
    import zlib

    import numpy as np

    out = dict(_drawn_inputs(seed))
    spreads = {'L0_attn_D': (1.0, 0.6), 'L0_attn_norm_w': (1.0, 0.6), 'L0_attn_norm_b': (0.0, 0.8)}
    factors = {'L0_attn_in_proj_w': 5.254,
     'L0_attn_conv_w': 3.771,
     'L0_attn_x_proj_w': 8.0,
     'L0_attn_dt_proj_w': 8.0,
     'L0_attn_dt_proj_b': 8.0,
     'L0_attn_A_log': 8.0,
     'L0_attn_out_proj_w': 4.832}
    for name, (base, spread) in spreads.items():
        noise = np.random.default_rng([zlib.crc32(name.encode()), seed]).standard_normal(out[name].shape)
        drawn = base * np.exp(spread * noise) if base else spread * noise
        out[name] = jnp.asarray(drawn.astype(out[name].dtype))
    for name, factor in factors.items():
        out[name] = (out[name] * factor).astype(out[name].dtype)
    return out
```

```python
from contextlib import ExitStack

import numpy as np
import concourse.bass as bass
from concourse import mybir
from concourse.alu_op_type import AluOpType as ALU

F32 = mybir.dt.float32
BF16 = mybir.dt.bfloat16
I32 = mybir.dt.int32
U32 = mybir.dt.uint32
ACT = mybir.ActivationFunctionType
AX = mybir.AxisListType
P = 128
EPS = 1e-5


def build(nc, x, winT, conv_w, xprojT, dt_w, dt_b, A_log, D, woutT, norm_w, norm_b,
          gate_w, sh_gate, sh_up, sh_down, rt_gate, rt_up, rt_down, out):
    NB, L, DIM = x.shape
    DIN = winT.shape[1]
    N = A_log.shape[1]
    TAPS = conv_w.shape[1]
    KC = DIM // P
    C = DIN // P
    J = L // P
    NT = NB * J
    TOK = NB * L
    E, _, FF = rt_gate.shape
    FC = FF // P
    SLOT_TILES = (TOK + E * (P - 1)) // P
    CL = C * L
    G3 = 2 * N

    x1_d = nc.dram_tensor("x1_rows", (TOK, DIM), F32).ap()
    xn_d = nc.dram_tensor("xn_rows", (TOK, DIM), F32).ap()
    xs_d = nc.dram_tensor("slot_in", (SLOT_TILES * P, DIM), F32).ap()
    y_d = nc.dram_tensor("slot_out", (SLOT_TILES * P, DIM), F32).ap()

    ctx = ExitStack()
    with ctx:
        def sb(name, shape, dt=F32, where=ctx):
            return where.enter_context(nc.sbuf_tensor(name, shape, dt))

        def sem(name):
            return ctx.enter_context(nc.semaphore(name))

        ps = [ctx.enter_context(nc.psum_tensor(f"bank{i}", [P, 512], F32)) for i in range(4, 8)]
        psY = ctx.enter_context(nc.psum_tensor("psY", [P, C, L], F32))
        psB, psC, psF, psG = ps

        ident = sb("ident", [P, P])
        xnT = sb("xnT", [P, KC, TOK])
        logits = sb("logits", [P, NT, E])
        epsc = sb("epsc", [P, 1])
        zrow = sb("zrow", [P, DIM])
        carrier = sb("carrier", [P, 1])

        A = ExitStack()
        ctx.enter_context(A)
        win = sb("win", [P, KC, DIN], where=A)
        cw = sb("cw", [P, C, TAPS], where=A)
        xp = sb("xp", [P, C, 1 + G3], where=A)
        w_dt = sb("w_dt", [P, C, P], where=A)
        w_bc = sb("w_bc", [P, C, 4, G3], where=A)
        dtw = sb("dtw", [P, C], where=A)
        dtb = sb("dtb", [P, C], where=A)
        alog = sb("alog", [P, C, N], where=A)
        aneg = sb("aneg", [P, C, N], where=A)
        dcol = sb("dcol", [P, C], where=A)
        wout = sb("wout", [P, C, DIM], where=A)
        nw = sb("nw", [P, KC], where=A)
        nb_ = sb("nb", [P, KC], where=A)
        gw = sb("gw", [P, KC, E], where=A)
        self_ = sb("sel_f", [P, G3], where=A)
        sel = sb("sel", [P, G3], BF16, where=A)
        decay = [sb(f"decay{i}", [P, C, L], where=A) for i in range(2)]
        bx = [sb(f"bx{i}", [P, C, L], where=A) for i in range(2)]
        st = [sb(f"state{i}", [P, C, L], where=A) for i in range(2)]
        dt = [sb(f"dt{i}", [P, C, L], where=A) for i in range(2)]
        xh = [sb(f"xh{i}", [P, C, L], where=A) for i in range(2)]
        acc = sb("acc", [P, C, L], where=A)
        tmp = sb("tmp", [P, C, L], where=A)
        yv = sb("yv", [P, C, L], where=A)
        bbc = [sb(f"bbc{i}", [P, L], where=A) for i in range(2)]
        parts = [sb(f"parts{i}", [P, L], BF16, where=A) for i in range(2)]
        rest = sb("rest", [P, L], where=A)
        xin = sb("xin", [P, J, DIM], where=A)
        xres = sb("xres", [P, J, DIM], where=A)
        h0 = [sb(f"h0_{i}", [P, J, DIM], where=A) for i in range(2)]
        h1 = sb("h1", [P, J, DIM], where=A)
        hT = sb("hT", [P, KC, L], where=A)
        ao = sb("ao", [P, J, DIM], where=A)
        x1 = sb("x1", [P, J, DIM], where=A)
        xn = sb("xn", [P, J, DIM], where=A)
        xnTb = sb("xnTb", [P, KC, L], where=A)
        bst = [sb(f"bst{i}", [P, J, 6], where=A) for i in range(4)]
        mv = [sb(f"mv{i}", [P, J, 2], where=A) for i in range(4)]
        lnv = [sb(f"lnv{i}", [P, J], where=A) for i in range(4)]
        rstd = [sb(f"rstd{i}", [P, J], where=A) for i in range(4)]
        A.close()

        M = ctx.enter_context(ExitStack())
        wg = sb("wg", [P, E, KC, FF], where=M)
        wu = sb("wu", [P, E, KC, FF], where=M)
        wd = sb("wd", [P, E, FC, DIM], where=M)
        shg = sb("shg", [P, KC, FF], where=M)
        shu = sb("shu", [P, KC, FF], where=M)
        shd = sb("shd", [P, FC, DIM], where=M)
        ysh = sb("ysh", [P, NT, DIM], where=M)
        sg = [sb(f"sg{i}", [P, FF], where=M) for i in range(2)]
        MS = ExitStack()
        ctx.enter_context(MS)
        actS = [sb(f"actS{i}", [P, FC, L], where=MS) for i in range(2)]
        MS.close()
        xsl = [sb(f"xsl{i}", [P, DIM], where=M) for i in range(2)]
        xsT = [sb(f"xsT{i}", [P, KC, P], where=M) for i in range(2)]
        actN = [sb(f"actN{i}", [P, FF], where=M) for i in range(2)]
        actT = [sb(f"actT{i}", [P, FC, P], where=M) for i in range(2)]
        yo = [sb(f"yo{i}", [P, DIM], where=M) for i in range(2)]
        fy = [sb(f"fy{i}", [P, DIM], where=M) for i in range(2)]
        R = ctx.enter_context(ExitStack())
        rt = {n: sb(n, [P, NT, E], where=R) for n in ("oh", "cnt", "incl", "q")}
        iotaE = sb("iotaE", [P, E], where=R)
        iotaEi = sb("iotaEi", [P, E], I32, where=R)
        iotaJ = sb("iotaJ", [1, SLOT_TILES], where=R)
        iotaJi = sb("iotaJi", [1, SLOT_TILES], I32, where=R)
        mx = sb("mx", [P, NT], where=R)
        mn = sb("mn", [P, NT], where=R)
        score = sb("score", [P, NT], where=R)
        slotf = sb("slotf", [P, NT], where=R)
        slot = sb("slot", [P, NT], I32, where=R)
        ti = sb("ti", [P, E], I32, where=R)
        tf = sb("tf", [P, E], where=R)
        tend = sb("tend", [P, E], where=R)
        tstart = sb("tstart", [P, E], where=R)
        onesT = sb("onesT", [P, NT], where=R)
        upper = sb("upper", [P, P], where=R)
        ones = sb("ones", [P, P], where=R)
        le = sb("le", [1, SLOT_TILES, E], where=R)
        exf = sb("exf", [1, SLOT_TILES], where=R)
        exi = sb("exi", [1, SLOT_TILES], I32, where=R)
        xrow = [sb(f"xrow{i}", [P, DIM], where=R) for i in range(2)]
        srow = [sb(f"srow{i}", [P, DIM], where=R) for i in range(2)]
        fst = sb("fst", [P, 2, 6], where=R)
        fmv = sb("fmv", [P, 2, 2], where=R)
        fln = sb("fln", [P, 2], where=R)
        frs = sb("frs", [P, 2], where=R)

        consts = sem("consts_loaded")
        slots_zeroed = sem("slots_zeroed")
        ident_made = sem("ident_made")
        setup = sem("setup")
        aexp = sem("aexp")
        zeroed = sem("zeroed")
        x_loaded = sem("x_loaded")
        xres_loaded = sem("xres_loaded")
        b_bcast = sem("b_bcast")
        c_bcast = sem("c_bcast")
        b_copied = sem("b_copied")
        decay_ready = sem("decay_ready")
        bx_ready = sem("bx_ready")
        scanned = sem("scanned")
        weighted = sem("weighted")
        summed = sem("summed")
        vf = sem("vector_front_chain")
        vb = sem("vector_back_chain")
        sf = sem("scalar_chain")
        mv_ready = [sem(f"mv_ready{i}") for i in range(4)]
        rs_ready = [sem(f"rs_ready{i}") for i in range(4)]
        h0_ready = sem("h0_ready")
        h1_ready = sem("h1_ready")
        h1T_ready = sem("h1T_ready")
        hT_ready = sem("hT_ready")
        inproj_ready = sem("inproj_ready")
        tap_done = sem("tap_done")
        conv_done = sem("conv_done")
        xh_ready = sem("xh_ready")
        dtin_ready = sem("dtin_ready")
        proj_ready = sem("proj_ready")
        z_done = sem("z_done")
        soft_ready = sem("soft_ready")
        parts_ready = sem("parts_ready")
        dt_ready = sem("dt_ready")
        yv_done = sem("yv_done")
        ys_ready = sem("ys_ready")
        oproj_ready = sem("oproj_ready")
        ao_done = sem("ao_done")
        x1_ready = sem("x1_ready")
        xn_ready = sem("xn_ready")
        xnT_ready = sem("xnT_ready")
        xnT_copied = sem("xnT_copied")
        logit_ready = sem("logit_ready")
        logit_kept = sem("logit_kept")
        x1_stored = sem("x1_stored")
        xn_stored = sem("xn_stored")
        xnT_kept = sem("xnT_kept")
        sh_loaded = sem("shared_weights_loaded")
        rt_loaded = sem("routed_weights_loaded")
        iotas = sem("iotas")
        rc = sem("routing_chain")
        oh_ready = sem("oh_ready")
        rank_ready = sem("rank_ready")
        mx_ready = sem("mx_ready")
        score_ready = sem("score_ready")
        slot_ready = sem("slot_ready")
        ex_ready = sem("ex_ready")
        xrow_loaded = [sem(f"xrow_loaded{i}") for i in range(2)]
        srow_ready = sem("srow_ready")
        scattered = [sem(f"scattered{i}") for i in range(2)]
        s_up = sem("shared_up_ready")
        s_silu = sem("shared_silu")
        s_act = sem("shared_act")
        s_down = sem("shared_down_ready")
        s_kept = sem("shared_kept")
        xsl_loaded = [sem(f"xsl_loaded{i}") for i in range(2)]
        xsT_ready = sem("xsT_ready")
        xsT_copied = sem("xsT_copied")
        r_up = sem("routed_up_ready")
        r_silu = sem("routed_silu")
        r_act = sem("routed_act")
        actT_ready = sem("actT_ready")
        actT_copied = sem("actT_copied")
        r_down = sem("routed_down_ready")
        yo_ready = sem("yo_ready")
        yo_stored = [sem(f"yo_stored{i}") for i in range(2)]
        gathered = [sem(f"gathered{i}") for i in range(2)]
        f_loaded = [sem(f"f_loaded{i}") for i in range(2)]
        f_chain = sem("final_chain")
        f_mv = sem("final_mv")
        f_rs = sem("final_rs")
        f_ready = sem("final_ready")
        f_stored = [sem(f"f_stored{i}") for i in range(2)]

        NCONST = 11
        xb_v = x.rearrange("b (j p) c -> b p j c", p=P)
        x1b_v = x1_d.rearrange("(b j p) c -> b p j c", p=P, j=J)
        xnb_v = xn_d.rearrange("(b j p) c -> b p j c", p=P, j=J)
        x1t_v = x1_d.rearrange("(t p) c -> t p c", p=P)
        xnt_v = xn_d.rearrange("(t p) c -> t p c", p=P)
        xst_v = xs_d.rearrange("(t p) c -> t p c", p=P)
        yt_v = y_d.rearrange("(t p) c -> t p c", p=P)
        out_v = out.rearrange("b (j p) c -> (b j) p c", p=P)

        def pick(v, i):
            return v[bass.ds(i, 1)].rearrange("a p c -> p (a c)") if len(v.shape) == 3 else \
                v[bass.ds(i, 1)].rearrange("a p j c -> p (a j) c")

        block = ctx.enter_context(nc.Block())

        @block.sync
        def _(sp):
            sp.dma_start(xin[:], xb_v[0]).then_inc(x_loaded, 16)
            for dst, src in (
                (win, winT.rearrange("(k p) n -> p k n", p=P)),
                (cw, conv_w.rearrange("(c p) k -> p c k", p=P)),
                (xp, xprojT.rearrange("(c p) r -> p c r", p=P)),
                (dtw, dt_w),
                (dtb, dt_b),
                (alog, A_log.rearrange("(c p) d -> p c d", p=P)),
                (dcol, D),
                (nw, norm_w),
                (nb_, norm_b),
                (gw, gate_w.rearrange("(k p) e -> p k e", p=P)),
                (wout, woutT.rearrange("(c p) n -> p c n", p=P)),
            ):
                sp.dma_start(dst[:], src).then_inc(consts, 16)
            sp.wait_ge(zeroed, 1)
            sp.dma_start(xs_d.rearrange("(t p) c -> p t c", p=P),
                         zrow[:].unsqueeze(1).broadcast_to([P, SLOT_TILES, DIM])).then_inc(slots_zeroed, 16)

            def back_dma(b):
                if not (isinstance(b, int) and b == 0):
                    sp.wait_ge(x1_stored, 16 * b)
                    sp.wait_ge(xn_stored, 16 * b)
                    sp.wait_ge(xnT_kept, 16 * b)
                    sp.wait_ge(x1_ready, b)
                sp.dma_start(xres[:], pick(xb_v, b)).then_inc(xres_loaded, 16)
                sp.wait_ge(x1_ready, b + 1)
                sp.dma_start(pick(x1b_v, b), x1[:]).then_inc(x1_stored, 16)
                sp.wait_ge(xn_ready, b + 1)
                sp.dma_start(pick(xnb_v, b), xn[:]).then_inc(xn_stored, 16)
                sp.wait_ge(xnT_copied, b + 1)
                sp.dma_start(xnT[:, :, bass.ds(b * L, L)], xnTb[:]).then_inc(xnT_kept, 16)

            def next_x(f):
                sp.wait_ge(h0_ready, f)
                sp.dma_start(xin[:], pick(xb_v, f)).then_inc(x_loaded, 16)

            next_x(1)
            next_x(2)
            back_dma(0)
            with sp.Fori(1, NB - 2) as b:
                next_x(b + 2)
                back_dma(b)
            back_dma(NB - 2)
            back_dma(NB - 1)

            sp.wait_ge(xnT_kept, 16 * NB)
            sp.wait_ge(x1_stored, 16 * NB)
            sp.wait_ge(xn_stored, 16 * NB)
            sp.wait_ge(logit_kept, NB)
            for dst, src in ((shg, sh_gate), (shu, sh_up), (shd, sh_down)):
                sp.dma_start(dst[:], src.rearrange("(k p) n -> p k n", p=P)).then_inc(sh_loaded, 16)
            for i in range(2):
                sp.dma_start(xrow[i][:], xnt_v[i]).then_inc(xrow_loaded[i], 16)
            with sp.Fori(2, NT - 1, 2) as t:
                for i in range(2):
                    sp.wait_ge(srow_ready, t + i - 1)
                    sp.dma_start(xrow[i][:], pick(xnt_v, t + i)).then_inc(xrow_loaded[i], 16)
            for e in range(E):
                sp.dma_start(wg[:, e], rt_gate[e].rearrange("(k p) n -> p k n", p=P)).then_inc(rt_loaded, 16)
                sp.dma_start(wu[:, e], rt_up[e].rearrange("(k p) n -> p k n", p=P)).then_inc(rt_loaded, 16)
                sp.dma_start(wd[:, e], rt_down[e].rearrange("(k p) n -> p k n", p=P)).then_inc(rt_loaded, 16)

            sp.wait_ge(scattered[0], 16 * (NT // 2))
            sp.wait_ge(scattered[1], 16 * (NT // 2))
            sp.wait_ge(s_kept, 2 * NB)
            sp.wait_ge(s_act, NB * FC)

            def load_slots(s, i):
                sp.dma_start(xsl[i][:], pick(xst_v, s)).then_inc(xsl_loaded[i], 16)

            def store_slots(s, i):
                sp.wait_ge(yo_ready, s + 1)
                sp.dma_start(pick(yt_v, s), yo[i][:]).then_inc(yo_stored[i], 16)

            load_slots(0, 0)
            load_slots(1, 1)
            with sp.Fori(0, SLOT_TILES - 4, 2) as s:
                for i in range(2):
                    sp.wait_ge(xsT_ready, s + i + 1)
                    load_slots(s + i + 2, i)
                    store_slots(s + i, i)
            for s in range(SLOT_TILES - 3, SLOT_TILES):
                if s + 2 < SLOT_TILES:
                    sp.wait_ge(xsT_ready, s + 1)
                    load_slots(s + 2, s % 2)
                store_slots(s, s % 2)

            def load_res(t, i):
                sp.dma_start(xrow[i][:], pick(x1t_v, t)).then_inc(f_loaded[i], 16)

            def store_out(t, i):
                sp.wait_ge(f_ready, t + 1)
                sp.dma_start(pick(out_v, t), srow[i][:]).then_inc(f_stored[i], 16)

            load_res(0, 0)
            load_res(1, 1)
            with sp.Fori(0, NT - 3, 2) as t:
                for i in range(2):
                    store_out(t + i, i)
                    load_res(t + i + 2, i)
            store_out(NT - 2, 0)
            store_out(NT - 1, 1)
            sp.wait_ge(f_stored[0], 16 * (NT // 2))
            sp.wait_ge(f_stored[1], 16 * (NT // 2))

        @block.gpsimd
        def _(pool):
            nc.gpsimd.memset(zrow[:], 0.0).then_inc(zeroed, 1)
            nc.gpsimd.memset(ident[:], 0.0).then_inc(ident_made, 1)
            pool.wait_ge(ident_made, 1)
            nc.gpsimd.affine_select(out=ident[:], in_=ident[:], compare_op=ALU.not_equal, fill=1.0, base=0,
                                    pattern=[[-1, P]], channel_multiplier=1).then_inc(ident_made, 1)

            def input_step(b, par, d):
                n = b * N + d
                if d == 0:
                    pool.wait_ge(xh_ready, b + 1)
                pool.wait_ge(b_copied, n + 1)
                if not (isinstance(n, int) and n < 2):
                    pool.wait_ge(scanned, n - 1)
                nc.gpsimd.tensor_tensor(bx[d % 2][:], xh[par][:],
                                        bbc[d % 2][:].unsqueeze(1).broadcast_to([P, C, L]),
                                        ALU.mult).then_inc(bx_ready, 1)

            for d in range(N):
                input_step(0, 0, d)
            with pool.Fori(1, NB - 2, 2) as b:
                for q in range(2):
                    for d in range(N):
                        input_step(b + q, (1 + q) % 2, d)
            for d in range(N):
                input_step(NB - 1, 1, d)

            pool.wait_ge(xnT_kept, 16 * NB)
            pool.wait_ge(logit_kept, NB)
            pool.wait_ge(x1_stored, 16 * NB)
            pool.wait_ge(xn_stored, 16 * NB)
            nc.gpsimd.iota(iotaEi[:], pattern=[[1, E]], base=-E, channel_multiplier=0)
            nc.gpsimd.iota(iotaJi[:], pattern=[[1, SLOT_TILES]], base=0, channel_multiplier=0)
            nc.gpsimd.memset(ones[:], 1.0)
            nc.gpsimd.memset(onesT[:], 1.0)
            nc.gpsimd.memset(upper[:], 1.0).then_inc(iotas, 1)
            pool.wait_ge(iotas, 1)
            nc.gpsimd.affine_select(out=upper[:], in_=upper[:], compare_op=ALU.is_gt, fill=0.0, base=0,
                                    pattern=[[1, P]], channel_multiplier=-1).then_inc(iotas, 1)

            pool.wait_ge(slot_ready, 1)
            pool.wait_ge(slots_zeroed, 16)
            for t in range(NT):
                pool.wait_ge(srow_ready, t + 1)
                nc.gpsimd.indirect_dma_start(
                    out=xs_d, out_offset=bass.IndirectOffsetOnAxis(slot[:, t:t + 1].bitcast(U32), 0),
                    in_=srow[t % 2][:], in_offset=None).then_inc(scattered[t % 2], 16)

            pool.wait_ge(yo_stored[0], 16 * ((SLOT_TILES + 1) // 2))
            pool.wait_ge(yo_stored[1], 16 * (SLOT_TILES // 2))
            for t in range(NT):
                if t >= 2:
                    pool.wait_ge(f_ready, t - 1)
                nc.gpsimd.indirect_dma_start(
                    out=fy[t % 2][:], out_offset=None, in_=y_d,
                    in_offset=bass.IndirectOffsetOnAxis(slot[:, t:t + 1].bitcast(U32), 0),
                ).then_inc(gathered[t % 2], 16)


        @block.scalar
        def _(act):
            act.wait_ge(consts, 16 * NCONST)
            nc.scalar.activation(alog[:], alog[:], ACT.Exp).then_inc(aexp, 1)
            act.wait_ge(setup, 1)

            def inv_std(i, b):
                act.wait_ge(mv_ready[i], b + 1)
                nc.scalar.activation(lnv[i][:], mv[i][:, :, 1], ACT.Ln, bias=epsc[:]).then_inc(rs_ready[i], 1)
                act.wait_ge(rs_ready[i], 2 * b + 1)
                nc.scalar.activation(rstd[i][:], lnv[i][:], ACT.Exp, scale=-0.5).then_inc(rs_ready[i], 1)

            def front(f, par, slot_):
                first = isinstance(f, int) and f == 0
                if slot_ == 3:
                    inv_std(0, f)
                if slot_ == 5:
                    inv_std(1, f)
                if slot_ == 8:
                    for k in range(KC):
                        act.wait_ge(h1T_ready, KC * f + k + 1)
                        if k == 0 and not first:
                            act.wait_ge(inproj_ready, C * f)
                        last = nc.scalar.activation(hT[:, k], (psF, psG)[k][:], ACT.Identity,
                                                    scale=nw[:, k:k + 1], bias=nb_[:, k:k + 1])
                    last.then_inc(hT_ready, 1)
                if slot_ in (9, 11):
                    for c in (0, 1) if slot_ == 9 else (2, 3):
                        act.wait_ge(inproj_ready, C * f + c + 1)
                        if c == 0 and not first:
                            act.wait_ge(dt_ready, f)
                        nc.scalar.activation(acc[:, c], (psF, psG)[c % 2][:], ACT.Identity,
                                             scale=cw[:, c, TAPS - 1:TAPS]).then_inc(tap_done, 1)
                if slot_ == 12:
                    act.wait_ge(conv_done, C * (f + 1))
                    if not (isinstance(f, int) and f < 2):
                        act.wait_ge(yv_done, f - 1)
                    nc.scalar.activation(xh[par][:], acc[:], ACT.Silu).then_inc(xh_ready, 1)
                if slot_ == 13:
                    act.wait_ge(dtin_ready, f + 1)
                    act.wait_ge(xh_ready, f + 1)
                    for c in range(C):
                        last = nc.scalar.activation(acc[:, c], psF[:], ACT.Identity,
                                                    scale=dtw[:, c:c + 1], bias=dtb[:, c:c + 1])
                    last.then_inc(z_done, 1)
                    act.wait_ge(z_done, f + 1)
                    nc.scalar.activation(tmp[:], acc[:], ACT.Abs).then_inc(sf, 1)
                    act.wait_ge(sf, 2 * f + 1)
                    nc.scalar.activation(tmp[:], tmp[:], ACT.Exp, scale=-1.0).then_inc(sf, 1)
                    act.wait_ge(sf, 2 * f + 2)
                    nc.scalar.activation(tmp[:], tmp[:], ACT.Ln, bias=1.0).then_inc(soft_ready, 1)

            def back(b, slot_):
                if slot_ == 1:
                    act.wait_ge(yv_done, b + 1)
                    nc.scalar.activation(yv[:], yv[:], ACT.Silu).then_inc(ys_ready, 1)
                if slot_ == 4:
                    inv_std(2, b)
                if slot_ == 5:
                    inv_std(3, b)
                if slot_ == 6:
                    for k in range(KC):
                        act.wait_ge(xnT_ready, KC * b + k + 1)
                        last = nc.scalar.activation(xnTb[:, k], (psF, psG)[k][:], ACT.Identity)
                    last.then_inc(xnT_copied, 1)

            def copy_b(n, par):
                act.wait_ge(b_bcast, n + 1)
                if not (isinstance(n, int) and n < 2):
                    act.wait_ge(bx_ready, n - 1)
                nc.scalar.activation(bbc[par][:], psB[:], ACT.Identity).then_inc(b_copied, 1)

            def iteration(i, par, do_front, do_back, last):
                for d in range(N):
                    n = i * N + d
                    if do_back:
                        back(i - 1, d)
                    if do_front:
                        front(i + 1, 1 - par, d)
                    if not (last and d == N - 1):
                        copy_b(n + 1, (d + 1) % 2)
                    if d == 0:
                        act.wait_ge(dt_ready, i + 1)
                    if not (isinstance(n, int) and n < 2):
                        act.wait_ge(scanned, n - 1)
                    for c in range(C):
                        e = nc.scalar.activation(decay[d % 2][:, c, 1:L], dt[par][:, c, 1:L], ACT.Exp,
                                                 scale=aneg[:, c, d:d + 1])
                    e.then_inc(decay_ready, 1)

            for s in range(N):
                front(0, 0, s)
            copy_b(0, 0)
            iteration(0, 0, True, False, False)
            with act.Fori(1, NB - 2, 2) as i:
                iteration(i, 1, True, True, False)
                iteration(i + 1, 0, True, True, False)
            iteration(NB - 1, 1, False, True, True)
            for s in range(N):
                back(NB - 1, s)

            act.wait_ge(mx_ready, 1)
            nc.scalar.activation(score[:], mx[:], ACT.Sigmoid).then_inc(score_ready, 1)

            def sh_silu(g, c):
                u = g * FC + c
                act.wait_ge(s_up, u + 1)
                if not (isinstance(u, int) and u < 2):
                    act.wait_ge(s_act, u - 1)
                nc.scalar.activation(sg[c % 2][:], psY[:, c % 2], ACT.Silu).then_inc(s_silu, 1)

            def sh_keep(g):
                for h in range(2):
                    act.wait_ge(s_down, 2 * g + h + 1)
                    nc.scalar.activation(ysh[:, bass.ds(g * J + 2 * h, 2), :].rearrange("p a c -> p (a c)"),
                                         (psF, psG)[h][:], ACT.Identity).then_inc(s_kept, 1)

            for c in range(FC):
                sh_silu(0, c)
            with act.Fori(1, NB) as g:
                for c in range(FC):
                    sh_silu(g, c)
                sh_keep(g - 1)
            sh_keep(NB - 1)

            def rt_silu(s, i):
                act.wait_ge(r_up, s + 1)
                if not (isinstance(s, int) and s < 2):
                    act.wait_ge(r_act, s - 1)
                nc.scalar.activation(sg[i][:], psY[:, i], ACT.Silu).then_inc(r_silu, 1)

            def rt_out(s, i):
                act.wait_ge(r_down, s + 1)
                if not (isinstance(s, int) and s < 2):
                    act.wait_ge(yo_stored[i], (s - i) * 8)
                nc.scalar.activation(yo[i][:], (psF, psG)[i][:, 0:DIM], ACT.Identity).then_inc(yo_ready, 1)

            act.wait_ge(s_kept, 2 * NB)
            rt_silu(0, 0)
            rt_silu(1, 1)
            rt_out(0, 0)
            rt_silu(2, 0)
            rt_out(1, 1)
            with act.Fori(2, SLOT_TILES - 2, 2) as s:
                for i in range(2):
                    if i == 0:
                        rt_silu(s + 1, 1)
                        rt_out(s, 0)
                    else:
                        rt_silu(s + 2, 0)
                        rt_out(s + 1, 1)
            rt_out(SLOT_TILES - 1, (SLOT_TILES - 1) % 2)

            def fin(t, i):
                act.wait_ge(f_mv, t + 1)
                nc.scalar.activation(fln[:, i:i + 1], fmv[:, i, 1:2], ACT.Ln, bias=epsc[:]).then_inc(f_rs, 1)
                act.wait_ge(f_rs, 2 * t + 1)
                nc.scalar.activation(frs[:, i:i + 1], fln[:, i:i + 1], ACT.Exp, scale=-0.5).then_inc(f_rs, 1)

            with act.Fori(0, NT - 1, 2) as t:
                fin(t, 0)
                fin(t + 1, 1)

        VF_PER = 8
        VB_PER = 3

        @block.vector
        def _(dve):
            nc.vector.memset(epsc[:], EPS)
            for i in range(2):
                nc.vector.memset(decay[i][:], 0.0)
            dve.wait_ge(consts, 16 * NCONST)
            nc.vector.tensor_copy(w_dt[:], xp[:, :, 0:1].broadcast_to([P, C, P]))
            for g in range(4):
                nc.vector.tensor_copy(w_bc[:, :, g, :], xp[:, :, 1:1 + G3])
            dve.wait_ge(ident_made, 2)
            nc.vector.tensor_tensor(self_[:], ident[:, 0:G3], ident[:, 64:64 + G3], ALU.add).then_inc(vf, 1)
            dve.wait_ge(vf, 1)
            nc.vector.tensor_tensor(sel[:], self_[:], ident[:, 96:96 + G3], ALU.add)
            dve.wait_ge(aexp, 1)
            nc.vector.tensor_scalar(aneg[:], alog[:], -1.0, None, ALU.mult).then_inc(setup, 1)
            VF0 = 1

            class Chain:

                def __init__(self, s, per, base):
                    self.s, self.per, self.base, self.n = s, per, base, 0

                def link(self, b, ins):
                    self.n += 1
                    ins.then_inc(self.s, 1)
                    dve.wait_ge(self.s, b * self.per + self.base + (self.n - 1) % self.per + 1)

            cf = Chain(vf, VF_PER, VF0)
            cb = Chain(vb, VB_PER, 0)

            def stats(i, chain, b, src):
                for j in range(J):
                    last = nc.vector.bn_stats(out=bst[i][:, j, :], in_=src[:, j, :])
                chain.link(b, last)
                nc.vector.memset(carrier[:], 0.0)
                for j in range(J):
                    last = nc.vector.bn_aggr(out=mv[i][:, j, :], in_=bst[i][:, j, :])
                last.then_inc(mv_ready[i], 1)

            def normed(i, b, dst, src):
                dve.wait_ge(rs_ready[i], 2 * (b + 1))
                dve.wait_ge(mv_ready[i], b + 1)
                for j in range(J):
                    last = nc.vector.tensor_scalar(dst[:, j, :], src[:, j, :], mv[i][:, j, 0:1],
                                                   rstd[i][:, j:j + 1], ALU.subtract, ALU.mult)
                return last

            def front(f, par, slot_):
                first = isinstance(f, int) and f == 0
                if slot_ == 2:
                    dve.wait_ge(x_loaded, 16 * (f + 1))
                    stats(0, cf, f, xin)
                if slot_ == 4:
                    normed(0, f, h0[par], xin).then_inc(h0_ready, 1)
                    dve.wait_ge(h0_ready, f + 1)
                    stats(1, cf, f, h0[par])
                if slot_ == 5:
                    if not first:
                        dve.wait_ge(h1T_ready, KC * f)
                    normed(1, f, h1, h0[par]).then_inc(h1_ready, 1)
                if slot_ in (9, 11):
                    pair = (0, 1) if slot_ == 9 else (2, 3)
                    dve.wait_ge(tap_done, C * f + pair[1] + 1)
                    for s in range(1, TAPS):
                        for c in pair:
                            last = nc.vector.scalar_tensor_tensor(
                                out=acc[:, c, s:L], in0=(psF, psG)[c % 2][:, 0:L - s],
                                scalar=cw[:, c, TAPS - 1 - s:TAPS - s], in1=acc[:, c, s:L],
                                op0=ALU.mult, op1=ALU.add)
                            if s == TAPS - 1:
                                last.then_inc(conv_done, 1)
                        if s < TAPS - 1:
                            cf.link(f, last)
                if slot_ == 13:
                    dve.wait_ge(proj_ready, f + 1)
                    cf.link(f, nc.vector.tensor_copy(parts[par][:], psG[:]))
                    last = nc.vector.tensor_tensor(rest[64:P], psG[64:P, :], parts[par][64:P], ALU.subtract)
                    cf.link(f, last)
                    nc.vector.tensor_copy(parts[par][64:P], rest[64:P]).then_inc(parts_ready, 1)
                    dve.wait_ge(parts_ready, 2 * f + 1)
                    nc.vector.tensor_tensor(parts[par][96:P], rest[96:P], parts[par][96:P],
                                            ALU.subtract).then_inc(parts_ready, 1)
                if slot_ == 14:
                    dve.wait_ge(soft_ready, f + 1)
                    nc.vector.scalar_tensor_tensor(out=dt[par][:], in0=acc[:], scalar=0.0, in1=tmp[:],
                                                   op0=ALU.max, op1=ALU.add).then_inc(dt_ready, 1)

            def back(b, par, slot_):
                if slot_ == 0:
                    dve.wait_ge(summed, N * (b + 1))
                    for c in range(C):
                        last = nc.vector.scalar_tensor_tensor(out=yv[:, c], in0=xh[par][:, c],
                                                              scalar=dcol[:, c:c + 1], in1=psY[:, c],
                                                              op0=ALU.mult, op1=ALU.add)
                    last.then_inc(yv_done, 1)
                if slot_ == 3:
                    for h in range(2):
                        dve.wait_ge(oproj_ready, 2 * b + h + 1)
                        last = nc.vector.tensor_tensor(ao[:, 2 * h:2 * h + 2].rearrange("p a c -> p (a c)"),
                                                       (psF, psG)[h][:],
                                                       h0[par][:, 2 * h:2 * h + 2].rearrange("p a c -> p (a c)"),
                                                       ALU.add)
                    last.then_inc(ao_done, 1)
                    dve.wait_ge(ao_done, b + 1)
                    stats(2, cb, b, ao)
                if slot_ == 4:
                    dve.wait_ge(xres_loaded, 16 * (b + 1))
                    cb.link(b, normed(2, b, x1, ao))
                    nc.vector.tensor_tensor(x1[:], x1[:], xres[:], ALU.add).then_inc(x1_ready, 1)
                    dve.wait_ge(x1_ready, b + 1)
                    stats(3, cb, b, x1)
                if slot_ == 5:
                    normed(3, b, xn, x1).then_inc(xn_ready, 1)
                if slot_ == 7:
                    dve.wait_ge(logit_ready, b + 1)
                    nc.vector.tensor_copy(logits[:, bass.ds(b * J, J), :].rearrange("p j e -> p (j e)"),
                                          psF[:, 0:J * E]).then_inc(logit_kept, 1)

            def iteration(i, par, do_front, do_back):
                for d in range(N):
                    n = i * N + d
                    dve.wait_ge(decay_ready, n + 1)
                    dve.wait_ge(bx_ready, n + 1)
                    if not (isinstance(n, int) and n < 2):
                        dve.wait_ge(summed, n - 1)
                    nc.vector.tensor_tensor_scan(st[d % 2][:].rearrange("p c t -> p (c t)"),
                                                 decay[d % 2][:].rearrange("p c t -> p (c t)"),
                                                 bx[d % 2][:].rearrange("p c t -> p (c t)"),
                                                 0.0, ALU.mult, ALU.add).then_inc(scanned, 1)
                    if do_back:
                        back(i - 1, 1 - par, d)
                    if do_front:
                        front(i + 1, 1 - par, d)
                    dve.wait_ge(c_bcast, n + 1)
                    dve.wait_ge(scanned, n + 1)
                    nc.vector.tensor_tensor(st[d % 2][:], st[d % 2][:],
                                            psC[:].unsqueeze(1).broadcast_to([P, C, L]),
                                            ALU.mult).then_inc(weighted, 1)

            for s in range(N):
                front(0, 0, s)
            iteration(0, 0, True, False)
            with dve.Fori(1, NB - 2, 2) as i:
                iteration(i, 1, True, True)
                iteration(i + 1, 0, True, True)
            iteration(NB - 1, 1, False, True)
            for s in range(N):
                back(NB - 1, 1, s)

            rn = [0]

            def link(ins):
                rn[0] += 1
                ins.then_inc(rc, 1)
                dve.wait_ge(rc, rn[0])

            def bt(a):
                return a.unsqueeze(2).broadcast_to([P, NT, E])

            def be(a):
                return a.unsqueeze(1).broadcast_to([P, NT, E])

            oh, cnt, incl, q = rt["oh"], rt["cnt"], rt["incl"], rt["q"]
            dve.wait_ge(iotas, 2)
            dve.wait_ge(logit_kept, NB)
            nc.vector.tensor_copy(iotaJ[:], iotaJi[:])
            link(nc.vector.tensor_copy(iotaE[:], iotaEi[:]))
            nc.vector.tensor_reduce(out=mx[:], in_=logits[:], axis=AX.X, op=ALU.max).then_inc(mx_ready, 1)
            dve.wait_ge(mx_ready, 1)
            link(nc.vector.tensor_tensor(q[:], logits[:], bt(mx[:]), ALU.is_equal))
            link(nc.vector.tensor_tensor(q[:], q[:], be(iotaE[:]), ALU.mult))
            link(nc.vector.tensor_reduce(out=mn[:], in_=q[:], axis=AX.X, op=ALU.min))
            nc.vector.tensor_tensor(oh[:], be(iotaE[:]), bt(mn[:]), ALU.is_equal).then_inc(oh_ready, 1)
            dve.wait_ge(rank_ready, 2)
            link(nc.vector.tensor_copy(cnt[:].rearrange("p t e -> p (t e)"), psC[:, 0:NT * E]))
            for e in range(E):
                last = nc.vector.tensor_tensor_scan(incl[:, :, e], onesT[:], cnt[:, :, e], 0.0, ALU.mult, ALU.add)
            link(last)
            link(nc.vector.tensor_tensor(q[:].rearrange("p t e -> p (t e)"), psB[:, 0:NT * E],
                                         incl[:].rearrange("p t e -> p (t e)"), ALU.add))
            link(nc.vector.tensor_tensor(q[:], q[:], cnt[:], ALU.subtract))
            link(nc.vector.tensor_scalar(ti[:], incl[:, NT - 1, :], float(P - 1), None, ALU.add))
            link(nc.vector.tensor_scalar(ti[:], ti[:], 7, None, ALU.arith_shift_right))
            link(nc.vector.tensor_copy(tf[:], ti[:]))
            link(nc.vector.tensor_tensor_scan(tend[:], onesT[:, 0:E], tf[:], 0.0, ALU.mult, ALU.add))
            link(nc.vector.tensor_tensor(tstart[:], tend[:], tf[:], ALU.subtract))
            link(nc.vector.tensor_scalar(tstart[:], tstart[:], float(P), None, ALU.mult))
            link(nc.vector.tensor_tensor(q[:], q[:], be(tstart[:]), ALU.add))
            link(nc.vector.tensor_tensor(q[:], q[:], oh[:], ALU.mult))
            link(nc.vector.tensor_reduce(out=slotf[:], in_=q[:], axis=AX.X, op=ALU.add))
            nc.vector.tensor_copy(slot[:], slotf[:]).then_inc(slot_ready, 1)
            link(nc.vector.tensor_tensor(le[:], tend[0:1, :].unsqueeze(1).broadcast_to([1, SLOT_TILES, E]),
                                         iotaJ[:].unsqueeze(2).broadcast_to([1, SLOT_TILES, E]), ALU.is_le))
            link(nc.vector.tensor_reduce(out=exf[:], in_=le[:], axis=AX.X, op=ALU.add))
            nc.vector.tensor_scalar(exi[:], exf[:], float(E - 1), None, ALU.min).then_inc(ex_ready, 1)

            def scale_rows(t, i):
                dve.wait_ge(xrow_loaded[i], 8 * (t - i) + 16)
                if not (isinstance(t, int) and t < 2):
                    dve.wait_ge(scattered[i], 8 * (t - i))
                nc.vector.tensor_scalar(srow[i][:], xrow[i][:], score[:, bass.ds(t, 1)], None,
                                        ALU.mult).then_inc(srow_ready, 1)

            def sh_act(g, gp, c):
                u = g * FC + c
                dve.wait_ge(s_silu, u + 1)
                if c == 0 and not (isinstance(g, int) and g < 2):
                    dve.wait_ge(s_down, 2 * (g - 1))
                nc.vector.tensor_tensor(actS[gp][:, c], sg[c % 2][:], psY[:, 2 + c % 2], ALU.mult).then_inc(s_act, 1)

            dve.wait_ge(score_ready, 1)
            for g in (0, 1):
                for c in range(FC):
                    sh_act(g, g, c)
                    scale_rows(g * FC + c, c % 2)
            with dve.Fori(2, NB - 1, 2) as g:
                for h in range(2):
                    for c in range(FC):
                        sh_act(g + h, h, c)
                        scale_rows((g + h) * FC + c, c % 2)

            def copy_xsT(s, i):
                dve.wait_ge(xsT_ready, s + 1)
                if not (isinstance(s, int) and s < 2):
                    dve.wait_ge(r_up, s - 1)
                nc.vector.tensor_copy(xsT[i][:].rearrange("p k t -> p (k t)"), psB[:, 0:KC * P]).then_inc(xsT_copied, 1)

            def rt_act(s, i):
                dve.wait_ge(r_silu, s + 1)
                if not (isinstance(s, int) and s < 2):
                    dve.wait_ge(actT_ready, s - 1)
                nc.vector.tensor_tensor(actN[i][:], sg[i][:], psY[:, 2 + i], ALU.mult).then_inc(r_act, 1)

            def copy_actT(s, i):
                dve.wait_ge(actT_ready, s + 1)
                if not (isinstance(s, int) and s < 2):
                    dve.wait_ge(r_down, s - 1)
                nc.vector.tensor_copy(actT[i][:].rearrange("p k t -> p (k t)"), psC[:]).then_inc(actT_copied, 1)

            S = SLOT_TILES
            dve.wait_ge(s_down, 2 * NB)
            copy_xsT(0, 0)
            copy_xsT(1, 1)
            rt_act(0, 0)
            for s in (0, 1):
                copy_xsT(s + 2, s % 2)
                copy_actT(s, s % 2)
                rt_act(s + 1, (s + 1) % 2)
            with dve.Fori(2, S - 4, 2) as s:
                for i in range(2):
                    copy_xsT(s + i + 2, i)
                    copy_actT(s + i, i)
                    rt_act(s + i + 1, 1 - i)
            for s in range(S - 3, S):
                if s + 2 < S:
                    copy_xsT(s + 2, s % 2)
                copy_actT(s, s % 2)
                if s + 1 < S:
                    rt_act(s + 1, (s + 1) % 2)

            def fin_sum(t, i):
                dve.wait_ge(gathered[i], 8 * (t - i) + 16)
                nc.vector.tensor_tensor(fy[i][:], fy[i][:], ysh[:, bass.ds(t, 1), :].rearrange("p a c -> p (a c)"),
                                        ALU.add).then_inc(f_chain, 1)
                dve.wait_ge(f_chain, 3 * t + 1)
                nc.vector.bn_stats(out=fst[:, i, :], in_=fy[i][:]).then_inc(f_chain, 1)
                dve.wait_ge(f_chain, 3 * t + 2)
                nc.vector.memset(carrier[:], 0.0)
                nc.vector.bn_aggr(out=fmv[:, i, :], in_=fst[:, i, :]).then_inc(f_mv, 1)

            def fin_out(t, i):
                dve.wait_ge(f_rs, 2 * (t + 1))
                dve.wait_ge(f_mv, t + 1)
                if not (isinstance(t, int) and t < 2):
                    dve.wait_ge(f_stored[i], 8 * (t - i))
                nc.vector.tensor_scalar(srow[i][:], fy[i][:], fmv[:, i, 0:1], frs[:, i:i + 1],
                                        ALU.subtract, ALU.mult).then_inc(f_chain, 1)
                dve.wait_ge(f_chain, 3 * (t + 1))
                dve.wait_ge(f_loaded[i], 8 * (t - i) + 16)
                nc.vector.tensor_tensor(srow[i][:], srow[i][:], xrow[i][:], ALU.add).then_inc(f_ready, 1)

            dve.wait_ge(scattered[0], 16 * (NT // 2))
            dve.wait_ge(scattered[1], 16 * (NT // 2))
            for t in (0, 1):
                fin_sum(t, t)
                fin_out(t, t)
            with dve.Fori(2, NT - 1, 2) as t:
                for i in range(2):
                    fin_sum(t + i, i)
                    fin_out(t + i, i)

        @block.tensor
        def _(pe):
            pe.wait_ge(ident_made, 2)
            pe.wait_ge(consts, 16 * NCONST)
            pe.wait_ge(setup, 1)

            def bcast_row(dst, par, r):
                return nc.tensor.matmul(dst[:], sel[:, r:r + 1].broadcast_to([P, P]), parts[par][:],
                                        start=True, stop=True)

            def bcast_b(n, par, d):
                if d == 0:
                    pe.wait_ge(parts_ready, 2 * (n // N + 1) if isinstance(n, int) else (n - 0) // 8 + 2)
                if not (isinstance(n, int) and n == 0):
                    pe.wait_ge(b_copied, n)
                bcast_row(psB, par, d).then_inc(b_bcast, 1)

            def bcast_c(n, par, d):
                if not (isinstance(n, int) and n == 0):
                    pe.wait_ge(weighted, n)
                bcast_row(psC, par, N + d).then_inc(c_bcast, 1)

            def front(f, par, slot_):
                first = isinstance(f, int) and f == 0
                if slot_ == 7:
                    pe.wait_ge(h1_ready, f + 1)
                    if not first:
                        pe.wait_ge(z_done, f)
                        pe.wait_ge(parts_ready, 2 * f)
                    if not (isinstance(f, int) and f < 2):
                        pe.wait_ge(logit_kept, f - 1)
                        pe.wait_ge(xnT_copied, f - 1)
                    for k in range(KC):
                        for j in range(J):
                            last = nc.tensor.transpose((psF, psG)[k][:, j * P:(j + 1) * P],
                                                       h1[:, j, k * P:(k + 1) * P], ident[:])
                        last.then_inc(h1T_ready, 1)
                if slot_ in (8, 10):
                    pe.wait_ge(hT_ready, f + 1)
                    for c in (0, 1) if slot_ == 8 else (2, 3):
                        if c >= 2:
                            pe.wait_ge(conv_done, C * f + c - 1)
                        for k in range(KC):
                            last = nc.tensor.matmul((psF, psG)[c % 2][:], win[:, k, c * P:(c + 1) * P], hT[:, k],
                                                    start=(k == 0), stop=(k == KC - 1))
                        last.then_inc(inproj_ready, 1)
                if slot_ == 12:
                    pe.wait_ge(xh_ready, f + 1)
                    pe.wait_ge(conv_done, C * (f + 1))
                    for c in range(C):
                        last = nc.tensor.matmul(psF[:], w_dt[:, c], xh[par][:, c], start=(c == 0), stop=(c == C - 1))
                    last.then_inc(dtin_ready, 1)
                    for c in range(C):
                        last = nc.tensor.matmul(psG[:], w_bc[:, c].rearrange("p g r -> p (g r)"), xh[par][:, c],
                                                start=(c == 0), stop=(c == C - 1))
                    last.then_inc(proj_ready, 1)

            def back(b, slot_, fronts):
                if slot_ == 2:
                    pe.wait_ge(ys_ready, b + 1)
                    pe.wait_ge(z_done, fronts)
                    pe.wait_ge(parts_ready, 2 * fronts)
                    if isinstance(b, int) and b == NB - 1:
                        pe.wait_ge(logit_kept, b)
                        pe.wait_ge(xnT_copied, b)
                    for j in range(J):
                        for c in range(C):
                            last = nc.tensor.matmul((psF, psG)[j // 2][:, (j % 2) * DIM:(j % 2 + 1) * DIM],
                                                    yv[:, c, j * P:(j + 1) * P], wout[:, c],
                                                    start=(c == 0), stop=(c == C - 1))
                        if j % 2:
                            last.then_inc(oproj_ready, 1)
                if slot_ == 5:
                    pe.wait_ge(xn_ready, b + 1)
                    pe.wait_ge(ao_done, b + 1)
                    for k in range(KC):
                        for j in range(J):
                            last = nc.tensor.transpose((psF, psG)[k][:, j * P:(j + 1) * P],
                                                       xn[:, j, k * P:(k + 1) * P], ident[:])
                        last.then_inc(xnT_ready, 1)
                if slot_ == 6:
                    pe.wait_ge(xnT_copied, b + 1)
                    for j in range(J):
                        for k in range(KC):
                            last = nc.tensor.matmul(psF[:, j * E:(j + 1) * E], xnTb[:, k, j * P:(j + 1) * P],
                                                    gw[:, k], start=(k == 0), stop=(k == KC - 1))
                    last.then_inc(logit_ready, 1)

            def iteration(i, par, do_front, do_back, last):
                for d in range(N):
                    n = i * N + d
                    if do_back:
                        back(i - 1, d, i + 1)
                    if do_front:
                        front(i + 1, 1 - par, d)
                    if not (last and d >= N - 2):
                        if d == N - 2:
                            pe.wait_ge(parts_ready, 2 * (i + 2))
                        pe.wait_ge(b_copied, n + 2)
                        bcast_row(psB, par if d < N - 2 else 1 - par, (d + 2) % N).then_inc(b_bcast, 1)
                    pe.wait_ge(weighted, n + 1)
                    if not (last and d == N - 1):
                        bcast_row(psC, par if d < N - 1 else 1 - par, N + (d + 1) % N).then_inc(c_bcast, 1)
                    if d == 0 and do_back:
                        pe.wait_ge(yv_done, i)
                    for c in range(C):
                        s = nc.tensor.matmul(psY[:, c], ident[:], st[d % 2][:, c], start=(d == 0), stop=(d == N - 1))
                    s.then_inc(summed, 1)

            for s in range(N):
                front(0, 0, s)
            pe.wait_ge(parts_ready, 2)
            bcast_row(psB, 0, 0).then_inc(b_bcast, 1)
            bcast_row(psC, 0, N).then_inc(c_bcast, 1)
            pe.wait_ge(b_copied, 1)
            bcast_row(psB, 0, 1).then_inc(b_bcast, 1)
            iteration(0, 0, True, False, False)
            with pe.Fori(1, NB - 2, 2) as i:
                iteration(i, 1, True, True, False)
                iteration(i + 1, 0, True, True, False)
            iteration(NB - 1, 1, False, True, True)
            for s in range(N):
                back(NB - 1, s, NB)

            pe.wait_ge(oh_ready, 1)
            oh = rt["oh"][:].rearrange("p t e -> p (t e)")
            nc.tensor.matmul(psB[:, 0:NT * E], upper[:], oh, start=True, stop=True).then_inc(rank_ready, 1)
            nc.tensor.matmul(psC[:, 0:NT * E], ones[:], oh, start=True, stop=True).then_inc(rank_ready, 1)

            def sh_up_(g, c):
                u = g * FC + c
                if not (isinstance(u, int) and u < 2):
                    pe.wait_ge(s_act, u - 1)
                for w, bank in ((shg, psY[:, c % 2]), (shu, psY[:, 2 + c % 2])):
                    for k in range(KC):
                        last = nc.tensor.matmul(bank, w[:, k, c * P:(c + 1) * P], xnT[:, k, bass.ds(g * L, L)],
                                                start=(k == 0), stop=(k == KC - 1))
                last.then_inc(s_up, 1)

            def sh_down_(g, gp):
                pe.wait_ge(s_act, (g + 1) * FC)
                for j in range(J):
                    if j % 2 == 0 and not (isinstance(g, int) and g == 0):
                        pe.wait_ge(s_kept, 2 * g + j // 2 - 1)
                    for c in range(FC):
                        last = nc.tensor.matmul((psF, psG)[j // 2][:, (j % 2) * DIM:(j % 2 + 1) * DIM],
                                                actS[gp][:, c, j * P:(j + 1) * P], shd[:, c],
                                                start=(c == 0), stop=(c == FC - 1))
                    if j % 2:
                        last.then_inc(s_down, 1)

            pe.wait_ge(sh_loaded, 48)
            pe.wait_ge(xnT_kept, 16 * NB)
            for g in (0, 1):
                for c in range(FC):
                    sh_up_(g, c)
            sh_down_(0, 0)
            with pe.Fori(2, NB - 1, 2) as g:
                for h in range(2):
                    for c in range(FC):
                        sh_up_(g + h, c)
                    sh_down_(g + h - 1, 1 - h)
            sh_down_(NB - 1, 1)

            def xsT_(s, i):
                pe.wait_ge(xsl_loaded[i], 8 * (s - i) + 16)
                if not (isinstance(s, int) and s == 0):
                    pe.wait_ge(xsT_copied, s)
                for k in range(KC):
                    last = nc.tensor.transpose(psB[:, k * P:(k + 1) * P], xsl[i][:, k * P:(k + 1) * P], ident[:])
                last.then_inc(xsT_ready, 1)

            def up_(s, i):
                pe.wait_ge(xsT_copied, s + 1)
                if not (isinstance(s, int) and s < 2):
                    pe.wait_ge(r_act, s - 1)
                for w, bank in ((wg, psY[:, i]), (wu, psY[:, 2 + i])):
                    for k in range(KC):
                        last = nc.tensor.matmul(bank, xsT[i][:, k], w[:, bass.ds(ereg[i], 1), k].rearrange("p a n -> p (a n)"),
                                                start=(k == 0), stop=(k == KC - 1))
                last.then_inc(r_up, 1)

            def actT_(s, i):
                pe.wait_ge(r_act, s + 1)
                if not (isinstance(s, int) and s == 0):
                    pe.wait_ge(actT_copied, s)
                for c in range(FC):
                    last = nc.tensor.transpose(psC[:, c * P:(c + 1) * P], actN[i][:, c * P:(c + 1) * P], ident[:])
                last.then_inc(actT_ready, 1)

            def down_(s, i):
                pe.wait_ge(actT_copied, s + 1)
                if not (isinstance(s, int) and s < 2):
                    pe.wait_ge(yo_ready, s - 1)
                for c in range(FC):
                    last = nc.tensor.matmul((psF, psG)[i][:, 0:DIM], actT[i][:, c],
                                            wd[:, bass.ds(ereg[i], 1), c].rearrange("p a n -> p (a n)"),
                                            start=(c == 0), stop=(c == FC - 1))
                last.then_inc(r_down, 1)

            S = SLOT_TILES
            ereg = [None, None]

            def expert(s, i):
                ereg[i] = pe.value_load(exi[0:1, bass.ds(s, 1)], min_val=0, max_val=E - 1)

            pe.wait_ge(ex_ready, 1)
            pe.wait_ge(rt_loaded, 16 * 3 * E)
            pe.wait_ge(s_kept, 2 * NB)
            xsT_(0, 0)
            xsT_(1, 1)
            expert(0, 0)
            up_(0, 0)

            def step(s, i, ahead, more):
                if ahead:
                    xsT_(s + 2, i)
                actT_(s, i)
                if more:
                    expert(s + 1, 1 - i)
                    up_(s + 1, 1 - i)
                expert(s, i)
                down_(s, i)

            step(0, 0, True, True)
            step(1, 1, True, True)
            with pe.Fori(2, S - 4, 2) as s:
                step(s, 0, True, True)
                step(s + 1, 1, True, True)
            for s in range(S - 3, S):
                step(s, s % 2, s + 2 < S, s + 1 < S)


def kernel(**inputs):
    import concourse.bacc as _bacc
    from concourse.bass_utils import run_bass_kernel_spmd as _run

    def given(name, transposed=False):
        a = np.asarray(inputs[name])
        return np.ascontiguousarray(a.T if transposed else a)

    def columns(name):
        return np.ascontiguousarray(np.asarray(inputs[name]).reshape(-1, P).T)

    data = {
        "x": given("L0_attn_x"),
        "winT": given("L0_attn_in_proj_w", True),
        "conv_w": given("L0_attn_conv_w"),
        "xprojT": given("L0_attn_x_proj_w", True),
        "dt_w": columns("L0_attn_dt_proj_w"),
        "dt_b": columns("L0_attn_dt_proj_b"),
        "A_log": given("L0_attn_A_log"),
        "D": columns("L0_attn_D"),
        "woutT": given("L0_attn_out_proj_w", True),
        "norm_w": columns("L0_attn_norm_w"),
        "norm_b": columns("L0_attn_norm_b"),
        "gate_w": given("L0_ffn_gate_w"),
        "sh_gate": given("L0_ffn_sh_gate"),
        "sh_up": given("L0_ffn_sh_up"),
        "sh_down": given("L0_ffn_sh_down"),
        "rt_gate": given("L0_ffn_rt_gate"),
        "rt_up": given("L0_ffn_rt_up"),
        "rt_down": given("L0_ffn_rt_down"),
    }
    nc = _bacc.Bacc("TRN2", target_bir_lowering=False, num_devices=1)
    args = [nc.dram_tensor(f"in_{n}", a.shape, mybir.dt.from_np(a.dtype), kind="ExternalInput").ap()
            for n, a in data.items()]
    res = nc.dram_tensor("result", data["x"].shape, F32, kind="ExternalOutput").ap()
    build(nc, *args, res)
    r = _run(nc, [{f"in_{n}": a for n, a in data.items()}], core_ids=[0])
    return r.results[0]["result"]
```

```python
from contextlib import ExitStack

import numpy as np
import concourse.bass as bass
from concourse import mybir
from concourse.alu_op_type import AluOpType as ALU

F32 = mybir.dt.float32
BF16 = mybir.dt.bfloat16
I32 = mybir.dt.int32
U32 = mybir.dt.uint32
ACT = mybir.ActivationFunctionType
AX = mybir.AxisListType
P = 128
EPS = 1e-5
HALF_ROOT = float(np.sqrt(0.5))
LN_MARGIN = 2e-9


def build(nc, x, winT, conv_w, xprojT, dt_w, dt_b, A_log, D, woutT, norm_w, norm_b,
          gate_w, sh_gate, sh_up, sh_down, rt_gate, rt_up, rt_down, out):
    NB, L, DIM = x.shape
    DIN = winT.shape[1]
    N = A_log.shape[1]
    TAPS = conv_w.shape[1]
    KC = DIM // P
    C = DIN // P
    J = L // P
    NT = NB * J
    TOK = NB * L
    E, _, FF = rt_gate.shape
    FC = FF // P
    SLOT_TILES = (TOK + E * (P - 1)) // P
    CL = C * L
    RING = 4
    G3 = 2 * N

    x1_d = nc.dram_tensor("x1_rows", (TOK, DIM), F32).ap()
    xn_d = nc.dram_tensor("xn_rows", (TOK, DIM), F32).ap()
    xnT_d = nc.dram_tensor("xn_columns", (NB, P, KC * L), F32).ap()
    xs_d = nc.dram_tensor("slot_in", (SLOT_TILES * P, DIM), F32).ap()
    y_d = nc.dram_tensor("slot_out", (SLOT_TILES * P, DIM), F32).ap()

    ctx = ExitStack()
    with ctx:
        def sb(name, shape, dt=F32, where=ctx):
            return where.enter_context(nc.sbuf_tensor(name, shape, dt))

        def sem(name):
            return ctx.enter_context(nc.semaphore(name))

        ps = [ctx.enter_context(nc.psum_tensor(f"bank{i}", [P, 512], F32)) for i in range(4, 8)]
        psY = ctx.enter_context(nc.psum_tensor("psY", [P, C, L], F32))
        psB, psC, psF, psG = ps

        ident = sb("ident", [P, P])
        logits = sb("logits", [P, NT, E])
        epsc = sb("epsc", [P, 1])
        mone = sb("mone", [P, 1])
        zrow = sb("zrow", [P, DIM])
        carrier = sb("carrier", [P, 1])

        A = ExitStack()
        ctx.enter_context(A)
        win = sb("win", [P, KC, DIN], where=A)
        cw = sb("cw", [P, C, TAPS], where=A)
        xp = sb("xp", [P, C, 1 + G3], where=A)
        w_dt = sb("w_dt", [P, C, P], where=A)
        w_bc = sb("w_bc", [P, C, 4, G3], where=A)
        dtw = sb("dtw", [P, C], where=A)
        dtb = sb("dtb", [P, C], where=A)
        alog = sb("alog", [P, C, N], where=A)
        aneg = sb("aneg", [P, C, N], where=A)
        dcol = sb("dcol", [P, C], where=A)
        wout = sb("wout", [P, C, DIM], where=A)
        nw = sb("nw", [P, KC], where=A)
        nb_ = sb("nb", [P, KC], where=A)
        gw = sb("gw", [P, KC, E], where=A)
        sel_f = sb("sel_f", [P, G3], where=A)
        sel = sb("sel", [P, G3], BF16, where=A)
        decay = [sb(f"decay{i}", [P, C, L], where=A) for i in range(RING)]
        st = [sb(f"state{i}", [P, C, L], where=A) for i in range(RING)]
        dt = [sb(f"dt{i}", [P, C, L], where=A) for i in range(2)]
        xh = [sb(f"xh{i}", [P, C, L], where=A) for i in range(2)]
        acc = sb("acc", [P, C, L], where=A)
        tmp = sb("tmp", [P, C, L], where=A)
        yv = sb("yv", [P, C, L], where=A)
        sq = sb("sq", [P, C, L], where=A)
        bbc = [sb(f"bbc{i}", [P, L], where=A) for i in range(2)]
        parts = [sb(f"parts{i}", [P, L], BF16, where=A) for i in range(2)]
        rest = sb("rest", [P, L], where=A)
        xin = sb("xin", [P, J, DIM], where=A)
        xres = sb("xres", [P, J, DIM], where=A)
        h0 = [sb(f"h0_{i}", [P, J, DIM], where=A) for i in range(2)]
        h1 = sb("h1", [P, J, DIM], where=A)
        hT = sb("hT", [P, KC, L], where=A)
        ao = h1
        x1 = sb("x1", [P, J, DIM], where=A)
        xn = sb("xn", [P, J, DIM], where=A)
        xnTb = sb("xnTb", [P, KC, L], where=A)
        bst = [sb(f"bst{i}", [P, J, 6], where=A) for i in range(4)]
        mv = [sb(f"mv{i}", [P, J, 2], where=A) for i in range(4)]
        lnv = [sb(f"lnv{i}", [P, J], where=A) for i in range(4)]
        rstd = [sb(f"rstd{i}", [P, J], where=A) for i in range(4)]
        A.close()

        M = ctx.enter_context(ExitStack())
        WG = ExitStack()
        ctx.enter_context(WG)
        wg = sb("wg", [P, E, KC, FF], where=WG)
        WG.close()
        fx = sb("fx", [P, NT, DIM], where=M)
        wu = sb("wu", [P, E, KC, FF], where=M)
        wd = sb("wd", [P, E, FC, DIM], where=M)
        shg = sb("shg", [P, KC, FF], where=M)
        shu = sb("shu", [P, KC, FF], where=M)
        shd = sb("shd", [P, FC, DIM], where=M)
        ysh = sb("ysh", [P, NT, DIM], where=M)
        sg = [sb(f"sg{i}", [P, FF], where=M) for i in range(2)]
        xg = [sb(f"xg{i}", [P, KC, L], where=M) for i in range(2)]
        xsl = [sb(f"xsl{i}", [P, DIM], where=M) for i in range(2)]
        xsT = [sb(f"xsT{i}", [P, KC, P], where=M) for i in range(2)]
        MS = ExitStack()
        ctx.enter_context(MS)
        actS = [sb(f"actS{i}", [P, FC, L], where=MS) for i in range(2)]
        MS.close()
        actN = [sb(f"actN{i}", [P, FF], where=M) for i in range(2)]
        actT = [sb(f"actT{i}", [P, FC, P], where=M) for i in range(2)]
        yo = [sb(f"yo{i}", [P, DIM], where=M) for i in range(2)]
        fy = [sb(f"fy{i}", [P, 2, DIM], where=M) for i in range(2)]
        R = ctx.enter_context(ExitStack())
        rt = {n: sb(n, [P, NT, E], where=R) for n in ("oh", "cnt", "incl", "q")}
        iotaE = sb("iotaE", [P, E], where=R)
        iotaEi = sb("iotaEi", [P, E], I32, where=R)
        iotaJ = sb("iotaJ", [1, SLOT_TILES], where=R)
        iotaJi = sb("iotaJi", [1, SLOT_TILES], I32, where=R)
        mx = sb("mx", [P, NT], where=R)
        mn = sb("mn", [P, NT], where=R)
        score = sb("score", [P, NT], where=R)
        slotf = sb("slotf", [P, NT], where=R)
        slot = sb("slot", [P, NT], I32, where=R)
        ti = sb("ti", [P, E], I32, where=R)
        tf = sb("tf", [P, E], where=R)
        tend = sb("tend", [P, E], where=R)
        tstart = sb("tstart", [P, E], where=R)
        onesT = sb("onesT", [P, NT], where=R)
        upper = sb("upper", [P, P], where=R)
        ones = sb("ones", [P, P], where=R)
        le = sb("le", [1, SLOT_TILES, E], where=R)
        exf = sb("exf", [1, SLOT_TILES], where=R)
        exi = sb("exi", [1, SLOT_TILES], I32, where=R)
        xrow = [sb(f"xrow{i}", [P, J, DIM], where=R) for i in range(2)]
        fst = [sb(f"fst{i}", [P, 2, 6], where=R) for i in range(2)]
        fmv = [sb(f"fmv{i}", [P, 2, 2], where=R) for i in range(2)]
        fln = [sb(f"fln{i}", [P, 2], where=R) for i in range(2)]
        frs = [sb(f"frs{i}", [P, 2], where=R) for i in range(2)]

        consts = sem("consts_loaded")
        slots_zeroed = sem("slots_zeroed")
        ident_made = sem("ident_made")
        setup = sem("setup")
        aexp = sem("aexp")
        zeroed = sem("zeroed")
        x_loaded = sem("x_loaded")
        xres_loaded = sem("xres_loaded")
        b_bcast = sem("b_bcast")
        c_bcast = sem("c_bcast")
        b_copied = sem("b_copied")
        decay_ready = sem("decay_ready")
        bx_ready = sem("bx_ready")
        scanned = sem("scanned")
        weighted = sem("weighted")
        summed = sem("summed")
        vf = sem("vector_front_chain")
        vb = sem("vector_back_chain")
        sf = sem("scalar_chain")
        mv_ready = [sem(f"mv_ready{i}") for i in range(4)]
        rs_ready = [sem(f"rs_ready{i}") for i in range(4)]
        h0_ready = sem("h0_ready")
        h1_ready = sem("h1_ready")
        h1T_ready = sem("h1T_ready")
        hT_ready = sem("hT_ready")
        inproj_ready = sem("inproj_ready")
        tap_done = sem("tap_done")
        conv_done = sem("conv_done")
        xh_ready = sem("xh_ready")
        dtin_ready = sem("dtin_ready")
        proj_ready = sem("proj_ready")
        z_done = sem("z_done")
        sq_ready = sem("sq_ready")
        soft_ready = sem("soft_ready")
        parts_ready = sem("parts_ready")
        dt_ready = sem("dt_ready")
        yv_done = sem("yv_done")
        ys_ready = sem("ys_ready")
        oproj_ready = sem("oproj_ready")
        ao_done = sem("ao_done")
        x1_ready = sem("x1_ready")
        xn_ready = sem("xn_ready")
        xnT_ready = sem("xnT_ready")
        xnT_copied = sem("xnT_copied")
        logit_ready = sem("logit_ready")
        logit_kept = sem("logit_kept")
        x1_stored = sem("x1_stored")
        xn_stored = sem("xn_stored")
        xnT_kept = sem("xnT_kept")
        sh_loaded = sem("shared_weights_loaded")
        rt_loaded = sem("routed_weights_loaded")
        iotas = sem("iotas")
        rc = sem("routing_chain")
        oh_ready = sem("oh_ready")
        rank_ready = sem("rank_ready")
        mx_ready = sem("mx_ready")
        score_ready = sem("score_ready")
        slot_ready = sem("slot_ready")
        ex_ready = sem("ex_ready")
        xrow_loaded = [sem(f"xrow_loaded{i}") for i in range(2)]
        xrow_scaled = sem("xrow_scaled")
        scattered = [sem(f"scattered{i}") for i in range(2)]
        xg_loaded = [sem(f"xg_loaded{i}") for i in range(2)]
        s_up = sem("shared_up_ready")
        s_silu = sem("shared_silu")
        s_act = sem("shared_act")
        s_down = sem("shared_down_ready")
        s_kept = sem("shared_kept")
        xsl_loaded = [sem(f"xsl_loaded{i}") for i in range(2)]
        xsT_ready = sem("xsT_ready")
        xsT_copied = sem("xsT_copied")
        r_up = sem("routed_up_ready")
        r_silu = sem("routed_silu")
        r_act = sem("routed_act")
        actT_ready = sem("actT_ready")
        actT_copied = sem("actT_copied")
        r_down = sem("routed_down_ready")
        yo_ready = sem("yo_ready")
        yo_stored = [sem(f"yo_stored{i}") for i in range(2)]
        gathered = [sem(f"gathered{i}") for i in range(2)]
        f_loaded = [sem(f"f_half_loaded{i}") for i in range(2)]
        f_chain = sem("final_chain")
        f_normed = sem("final_normed")
        f_mv = sem("final_mv")
        f_rs = sem("final_rs")
        f_ready = sem("final_ready")
        f_stored = [sem(f"f_stored{i}") for i in range(2)]

        NCONST = 11
        xb_v = x.rearrange("b (j p) c -> b p j c", p=P)
        x1b_v = x1_d.rearrange("(b j p) c -> b p j c", p=P, j=J)
        xnb_v = xn_d.rearrange("(b j p) c -> b p j c", p=P, j=J)
        x1t_v = x1_d.rearrange("(t p) c -> p t c", p=P)
        xst_v = xs_d.rearrange("(t p) c -> t p c", p=P)
        yt_v = y_d.rearrange("(t p) c -> t p c", p=P)
        outp_v = out.rearrange("b (q h p) c -> (b q) p h c", p=P, h=2)

        def pick(v, i):
            return v[bass.ds(i, 1)].rearrange("a p c -> p (a c)") if len(v.shape) == 3 else \
                v[bass.ds(i, 1)].rearrange("a p j c -> p (a j) c")

        block = ctx.enter_context(nc.Block())

        @block.sync
        def _(sp):
            sp.dma_start(xin[:], xb_v[0]).then_inc(x_loaded, 16)
            for dst, src in (
                (win, winT.rearrange("(k p) n -> p k n", p=P)),
                (cw, conv_w.rearrange("(c p) k -> p c k", p=P)),
                (xp, xprojT.rearrange("(c p) r -> p c r", p=P)),
                (dtw, dt_w),
                (dtb, dt_b),
                (alog, A_log.rearrange("(c p) d -> p c d", p=P)),
                (dcol, D),
                (nw, norm_w),
                (nb_, norm_b),
                (gw, gate_w.rearrange("(k p) e -> p k e", p=P)),
                (wout, woutT.rearrange("(c p) n -> p c n", p=P)),
            ):
                sp.dma_start(dst[:], src).then_inc(consts, 16)
            sp.wait_ge(zeroed, 1)
            sp.dma_start(xs_d.rearrange("(t p) c -> p t c", p=P),
                         zrow[:].unsqueeze(1).broadcast_to([P, SLOT_TILES, DIM])).then_inc(slots_zeroed, 16)

            def back_dma(b):
                if not (isinstance(b, int) and b == 0):
                    sp.wait_ge(x1_stored, 16 * b)
                    sp.wait_ge(xn_stored, 16 * b)
                    sp.wait_ge(xnT_kept, 16 * b)
                    sp.wait_ge(x1_ready, b)
                sp.dma_start(xres[:], pick(xb_v, b)).then_inc(xres_loaded, 16)
                sp.wait_ge(x1_ready, b + 1)
                sp.dma_start(pick(x1b_v, b), x1[:]).then_inc(x1_stored, 16)
                sp.wait_ge(xn_ready, b + 1)
                sp.dma_start(pick(xnb_v, b), xn[:]).then_inc(xn_stored, 16)
                sp.wait_ge(xnT_copied, b + 1)
                sp.dma_start(xnT_d[bass.ds(b, 1)].rearrange("a p c -> p (a c)"),
                             xnTb[:].rearrange("p k t -> p (k t)")).then_inc(xnT_kept, 16)

            def next_x(f):
                sp.wait_ge(h0_ready, f)
                sp.dma_start(xin[:], pick(xb_v, f)).then_inc(x_loaded, 16)

            next_x(1)
            next_x(2)
            back_dma(0)
            with sp.Fori(1, NB - 2) as b:
                next_x(b + 2)
                back_dma(b)
            back_dma(NB - 2)
            back_dma(NB - 1)

            sp.wait_ge(xnT_kept, 16 * NB)
            sp.wait_ge(x1_stored, 16 * NB)
            sp.wait_ge(xn_stored, 16 * NB)
            sp.wait_ge(logit_kept, NB)
            for dst, src in ((shg, sh_gate), (shu, sh_up), (shd, sh_down)):
                sp.dma_start(dst[:], src.rearrange("(k p) n -> p k n", p=P)).then_inc(sh_loaded, 16)
            for g in (0, 1):
                sp.dma_start(xg[g][:].rearrange("p k t -> p (k t)"), xnT_d[g]).then_inc(xg_loaded[g], 16)
            for i in range(2):
                sp.dma_start(xrow[i][:], xnb_v[i]).then_inc(xrow_loaded[i], 16)
            for e in range(E):
                sp.dma_start(wg[:, e], rt_gate[e].rearrange("(k p) n -> p k n", p=P)).then_inc(rt_loaded, 16)
                sp.dma_start(wu[:, e], rt_up[e].rearrange("(k p) n -> p k n", p=P)).then_inc(rt_loaded, 16)
                sp.dma_start(wd[:, e], rt_down[e].rearrange("(k p) n -> p k n", p=P)).then_inc(rt_loaded, 16)

            for b in range(2, NB):
                sp.wait_ge(scattered[b % 2], 16 * J * (b // 2))
                sp.dma_start(xrow[b % 2][:], xnb_v[b]).then_inc(xrow_loaded[b % 2], 16)

            sp.wait_ge(scattered[0], 16 * (NT // 2))
            sp.wait_ge(scattered[1], 16 * (NT // 2))

            def load_slots(s, i):
                sp.dma_start(xsl[i][:], pick(xst_v, s)).then_inc(xsl_loaded[i], 16)

            load_slots(0, 0)
            load_slots(1, 1)
            with sp.Fori(0, SLOT_TILES - 4, 2) as s:
                for i in range(2):
                    sp.wait_ge(xsT_ready, s + i + 1)
                    load_slots(s + i + 2, i)
            for s in range(SLOT_TILES - 3, SLOT_TILES - 2):
                sp.wait_ge(xsT_ready, s + 1)
                load_slots(s + 2, s % 2)

            sp.wait_ge(r_up, SLOT_TILES)
            sp.wait_ge(x1_stored, 16 * NB)
            for h in range(2):
                for g in range(NB // 2):
                    rows = slice((h * NB // 2 + g) * J, (h * NB // 2 + g + 1) * J)
                    sp.dma_start(fx[:, rows, :], x1t_v[:, rows, :]).then_inc(f_loaded[h], 16)

            def store_out(q, i):
                sp.wait_ge(f_ready, q + 1)
                sp.dma_start(outp_v[bass.ds(q, 1)].rearrange("a p h c -> p (a h) c"),
                             fx[:, bass.ds(2 * q, 2), :]).then_inc(f_stored[i], 16)

            NQ = NT // 2
            with sp.Fori(0, NQ - 1, 2) as q:
                for i in range(2):
                    store_out(q + i, i)
            sp.wait_ge(f_stored[0], 16 * (NQ // 2))
            sp.wait_ge(f_stored[1], 16 * (NQ // 2))

        @block.gpsimd
        def _(pool):
            nc.gpsimd.memset(zrow[:], 0.0).then_inc(zeroed, 1)
            nc.gpsimd.memset(ident[:], 0.0).then_inc(ident_made, 1)
            pool.wait_ge(ident_made, 1)
            nc.gpsimd.affine_select(out=ident[:], in_=ident[:], compare_op=ALU.not_equal, fill=1.0, base=0,
                                    pattern=[[-1, P]], channel_multiplier=1).then_inc(ident_made, 1)

            def input_step(b, par, d):
                n = b * N + d
                if d == 0:
                    pool.wait_ge(xh_ready, b + 1)
                pool.wait_ge(b_copied, n + 1)
                if not (isinstance(n, int) and n < RING):
                    pool.wait_ge(summed, n - RING + 1)
                nc.gpsimd.tensor_tensor(st[d % RING][:], xh[par][:],
                                        bbc[d % 2][:].unsqueeze(1).broadcast_to([P, C, L]),
                                        ALU.mult).then_inc(bx_ready, 1)

            for d in range(N):
                input_step(0, 0, d)
            with pool.Fori(1, NB - 2, 2) as b:
                for q in range(2):
                    for d in range(N):
                        input_step(b + q, (1 + q) % 2, d)
            for d in range(N):
                input_step(NB - 1, 1, d)

            pool.wait_ge(xnT_kept, 16 * NB)
            pool.wait_ge(logit_kept, NB)
            pool.wait_ge(x1_stored, 16 * NB)
            pool.wait_ge(xn_stored, 16 * NB)
            nc.gpsimd.iota(iotaEi[:], pattern=[[1, E]], base=-E, channel_multiplier=0)
            nc.gpsimd.iota(iotaJi[:], pattern=[[1, SLOT_TILES]], base=0, channel_multiplier=0)
            nc.gpsimd.memset(ones[:], 1.0)
            nc.gpsimd.memset(onesT[:], 1.0)
            nc.gpsimd.memset(upper[:], 1.0).then_inc(iotas, 1)
            pool.wait_ge(iotas, 1)
            nc.gpsimd.affine_select(out=upper[:], in_=upper[:], compare_op=ALU.is_gt, fill=0.0, base=0,
                                    pattern=[[1, P]], channel_multiplier=-1).then_inc(iotas, 1)

            pool.wait_ge(score_ready, 1)
            pool.wait_ge(slot_ready, 1)
            pool.wait_ge(slots_zeroed, 16)
            for b in range(NB):
                pool.wait_ge(xrow_loaded[b % 2], 16 * (b // 2 + 1))
                nc.gpsimd.tensor_tensor(xrow[b % 2][:], xrow[b % 2][:],
                                        score[:, b * J:(b + 1) * J].unsqueeze(2).broadcast_to([P, J, DIM]),
                                        ALU.mult).then_inc(xrow_scaled, 1)
                pool.wait_ge(xrow_scaled, b + 1)
                for j in range(J):
                    t = b * J + j
                    nc.gpsimd.indirect_dma_start(
                        out=xs_d, out_offset=bass.IndirectOffsetOnAxis(slot[:, t:t + 1].bitcast(U32), 0),
                        in_=xrow[b % 2][:, j, :], in_offset=None).then_inc(scattered[b % 2], 16)

            pool.wait_ge(yo_stored[0], 16 * ((SLOT_TILES + 1) // 2))
            pool.wait_ge(yo_stored[1], 16 * (SLOT_TILES // 2))
            for t in range(NT):
                q = t // 2
                if t % 2 == 0 and q >= 2:
                    pool.wait_ge(f_ready, q - 1)
                nc.gpsimd.indirect_dma_start(
                    out=fy[q % 2][:, t % 2, :], out_offset=None, in_=y_d,
                    in_offset=bass.IndirectOffsetOnAxis(slot[:, t:t + 1].bitcast(U32), 0),
                ).then_inc(gathered[q % 2], 16)


        @block.scalar
        def _(act):
            def ln_exp_tables():
                nc.scalar.preload_act_table_set("natural_log_exp_and_others")

            ln_exp_tables()
            act.wait_ge(consts, 16 * NCONST)
            nc.scalar.activation(alog[:], alog[:], ACT.Exp).then_inc(aexp, 1)
            act.wait_ge(setup, 1)

            def inv_std(i, b):
                act.wait_ge(mv_ready[i], b + 1)
                nc.scalar.activation(lnv[i][:], mv[i][:, :, 1], ACT.Ln, bias=epsc[:]).then_inc(rs_ready[i], 1)
                act.wait_ge(rs_ready[i], 2 * b + 1)
                nc.scalar.activation(rstd[i][:], lnv[i][:], ACT.Exp, scale=-0.5).then_inc(rs_ready[i], 1)

            def front(f, par, slot_):
                first = isinstance(f, int) and f == 0
                if slot_ == 2:
                    inv_std(0, f)
                if slot_ == 4:
                    inv_std(1, f)
                if slot_ == 5:
                    for k in range(KC):
                        act.wait_ge(h1T_ready, KC * f + k + 1)
                        if k == 0 and not first:
                            act.wait_ge(inproj_ready, C * f)
                        last = nc.scalar.activation(hT[:, k], (psF, psG)[k][:], ACT.Identity,
                                                    scale=nw[:, k:k + 1], bias=nb_[:, k:k + 1])
                    last.then_inc(hT_ready, 1)
                if slot_ in (6, 7):
                    for c in (0, 1) if slot_ == 6 else (2, 3):
                        act.wait_ge(inproj_ready, C * f + c + 1)
                        if c == 0 and not first:
                            act.wait_ge(dt_ready, f)
                        nc.scalar.activation(acc[:, c], (psF, psG)[c % 2][:], ACT.Identity,
                                             scale=cw[:, c, TAPS - 1:TAPS])
                        nc.scalar.activation(sq[:, c], (psF, psG)[c % 2][:], ACT.Identity).then_inc(tap_done, 1)
                if slot_ == 9:
                    act.wait_ge(conv_done, C * (f + 1))
                    if not (isinstance(f, int) and f < 2):
                        act.wait_ge(yv_done, f - 1)
                    nc.scalar.activation(xh[par][:], acc[:], ACT.Silu).then_inc(xh_ready, 1)
                    ln_exp_tables()
                if slot_ == 11:
                    act.wait_ge(dtin_ready, f + 1)
                    act.wait_ge(xh_ready, f + 1)
                    for c in range(C):
                        last = nc.scalar.activation(acc[:, c], psF[:], ACT.Identity,
                                                    scale=dtw[:, c:c + 1], bias=dtb[:, c:c + 1])
                    last.then_inc(z_done, 1)
                    act.wait_ge(z_done, f + 1)
                    nc.scalar.activation(tmp[:], acc[:], ACT.Abs).then_inc(sf, 1)
                    act.wait_ge(sf, 4 * f + 1)
                    nc.scalar.activation(tmp[:], tmp[:], ACT.Exp, scale=-1.0).then_inc(sf, 1)
                if slot_ == 12:
                    act.wait_ge(sf, 4 * f + 2)
                    nc.scalar.activation(sq[:], tmp[:], ACT.Square, scale=HALF_ROOT).then_inc(sq_ready, 1)
                    if not (isinstance(f, int) and f < 2):
                        act.wait_ge(oproj_ready, 2 * f - 2)
                    nc.scalar.activation(yv[:], tmp[:], ACT.Identity, bias=1.0).then_inc(sf, 1)
                    act.wait_ge(sf, 4 * f + 3)
                    nc.scalar.activation(yv[:], yv[:], ACT.Identity, bias=mone[:]).then_inc(sf, 1)
                    act.wait_ge(sf, 4 * f + 4)
                    nc.scalar.activation(dt[par][:], yv[:], ACT.Ln, bias=1.0).then_inc(soft_ready, 1)

            def back(b, slot_):
                if slot_ == 1:
                    act.wait_ge(yv_done, b + 1)
                    nc.scalar.activation(yv[:], yv[:], ACT.Silu).then_inc(ys_ready, 1)
                    ln_exp_tables()
                if slot_ == 4:
                    inv_std(2, b)
                if slot_ == 5:
                    inv_std(3, b)
                if slot_ == 8:
                    for k in range(KC):
                        act.wait_ge(xnT_ready, KC * b + k + 1)
                        last = nc.scalar.activation(xnTb[:, k], (psF, psG)[k][:], ACT.Identity)
                    last.then_inc(xnT_copied, 1)

            def copy_b(n, par):
                act.wait_ge(b_bcast, n + 1)
                if not (isinstance(n, int) and n < 2):
                    act.wait_ge(bx_ready, n - 1)
                nc.scalar.activation(bbc[par][:], psB[:], ACT.Identity).then_inc(b_copied, 1)

            def iteration(i, par, do_front, do_back):
                for d in range(N):
                    n = i * N + d
                    if d == 0:
                        act.wait_ge(dt_ready, i + 1)
                    if not (isinstance(n, int) and n < RING):
                        act.wait_ge(scanned, n - RING + 1)
                    for c in range(C):
                        e = nc.scalar.activation(decay[d % RING][:, c, 1:L], dt[par][:, c, 1:L], ACT.Exp,
                                                 scale=aneg[:, c, d:d + 1])
                    e.then_inc(decay_ready, 1)
                    copy_b(n, d % 2)
                    if do_back:
                        back(i - 1, d)
                    if do_front:
                        front(i + 1, 1 - par, d)

            for s in range(N):
                front(0, 0, s)
            iteration(0, 0, True, False)
            with act.Fori(1, NB - 2, 2) as i:
                iteration(i, 1, True, True)
                iteration(i + 1, 0, True, True)
            iteration(NB - 1, 1, False, True)
            for s in range(N):
                back(NB - 1, s)

            act.wait_ge(mx_ready, 1)
            nc.scalar.activation(score[:], mx[:], ACT.Sigmoid).then_inc(score_ready, 1)

            def sh_silu(g, c):
                u = g * FC + c
                act.wait_ge(s_up, u + 1)
                if not (isinstance(u, int) and u < 2):
                    act.wait_ge(s_act, u - 1)
                nc.scalar.activation(sg[c % 2][:], psY[:, c % 2], ACT.Silu).then_inc(s_silu, 1)

            def sh_keep(g):
                for h in range(2):
                    act.wait_ge(s_down, 2 * g + h + 1)
                    nc.scalar.activation(ysh[:, bass.ds(g * J + 2 * h, 2), :].rearrange("p a c -> p (a c)"),
                                         (psF, psG)[h][:], ACT.Identity).then_inc(s_kept, 1)

            for c in range(FC):
                sh_silu(0, c)
            def load_group(g, i):
                act.wait_ge(s_up, (g - 1) * FC)
                act.dma_start(xg[i][:].rearrange("p k t -> p (k t)"),
                              xnT_d[bass.ds(g, 1)].rearrange("a p c -> p (a c)")).then_inc(xg_loaded[i], 16)

            load_group(2, 0)
            for c in range(FC):
                sh_silu(1, c)
            load_group(3, 1)
            sh_keep(0)
            with act.Fori(2, NB - 3, 2) as g:
                for h in range(2):
                    for c in range(FC):
                        sh_silu(g + h, c)
                    load_group(g + h + 2, h)
                    sh_keep(g + h - 1)
            for g in (NB - 2, NB - 1):
                for c in range(FC):
                    sh_silu(g, c)
                sh_keep(g - 1)
            sh_keep(NB - 1)

            def rt_silu(s, i):
                act.wait_ge(r_up, s + 1)
                if not (isinstance(s, int) and s < 2):
                    act.wait_ge(r_act, s - 1)
                nc.scalar.activation(sg[i][:], psY[:, i], ACT.Silu).then_inc(r_silu, 1)

            def rt_out(s, i):
                act.wait_ge(r_down, s + 1)
                if not (isinstance(s, int) and s < 2):
                    act.wait_ge(yo_stored[i], (s - i) * 8)
                nc.scalar.activation(yo[i][:], (psF, psG)[i][:, 0:DIM], ACT.Identity).then_inc(yo_ready, 1)
                act.wait_ge(yo_ready, s + 1)
                act.dma_start(pick(yt_v, s), yo[i][:]).then_inc(yo_stored[i], 16)

            act.wait_ge(s_kept, 2 * NB)
            rt_silu(0, 0)
            rt_silu(1, 1)
            rt_out(0, 0)
            rt_silu(2, 0)
            rt_out(1, 1)
            with act.Fori(2, SLOT_TILES - 2, 2) as s:
                for i in range(2):
                    if i == 0:
                        rt_silu(s + 1, 1)
                        rt_out(s, 0)
                    else:
                        rt_silu(s + 2, 0)
                        rt_out(s + 1, 1)
            rt_out(SLOT_TILES - 1, (SLOT_TILES - 1) % 2)

            ln_exp_tables()

            def fin(q, i):
                act.wait_ge(f_mv, q + 1)
                nc.scalar.activation(fln[i][:], fmv[i][:, :, 1], ACT.Ln, bias=epsc[:]).then_inc(f_rs, 1)
                act.wait_ge(f_rs, 2 * q + 1)
                nc.scalar.activation(frs[i][:], fln[i][:], ACT.Exp, scale=-0.5).then_inc(f_rs, 1)

            with act.Fori(0, NT // 2 - 1, 2) as q:
                fin(q, 0)
                fin(q + 1, 1)

        VF_PER = 11
        VB_PER = 3

        @block.vector
        def _(dve):
            nc.vector.memset(epsc[:], EPS)
            nc.vector.memset(mone[:], -1.0)
            for i in range(RING):
                nc.vector.memset(decay[i][:], 0.0)
            dve.wait_ge(consts, 16 * NCONST)
            nc.vector.tensor_copy(w_dt[:], xp[:, :, 0:1].broadcast_to([P, C, P]))
            for g in range(4):
                nc.vector.tensor_copy(w_bc[:, :, g, :], xp[:, :, 1:1 + G3])
            dve.wait_ge(ident_made, 2)
            nc.vector.tensor_tensor(sel_f[:], ident[:, 0:G3], ident[:, 64:64 + G3], ALU.add).then_inc(vf, 1)
            dve.wait_ge(vf, 1)
            nc.vector.tensor_tensor(sel[:], sel_f[:], ident[:, 96:96 + G3], ALU.add)
            dve.wait_ge(aexp, 1)
            nc.vector.tensor_scalar(aneg[:], alog[:], -1.0, None, ALU.mult).then_inc(setup, 1)
            VF0 = 1

            class Chain:

                def __init__(self, s, per, base):
                    self.s, self.per, self.base, self.n = s, per, base, 0

                def link(self, b, ins):
                    self.n += 1
                    ins.then_inc(self.s, 1)
                    dve.wait_ge(self.s, b * self.per + self.base + (self.n - 1) % self.per + 1)

            cf = Chain(vf, VF_PER, VF0)
            cb = Chain(vb, VB_PER, 0)

            def stats(i, chain, b, src):
                for j in range(J):
                    last = nc.vector.bn_stats(out=bst[i][:, j, :], in_=src[:, j, :])
                chain.link(b, last)
                nc.vector.memset(carrier[:], 0.0)
                for j in range(J):
                    last = nc.vector.bn_aggr(out=mv[i][:, j, :], in_=bst[i][:, j, :])
                last.then_inc(mv_ready[i], 1)

            def normed(i, b, dst, src):
                dve.wait_ge(rs_ready[i], 2 * (b + 1))
                dve.wait_ge(mv_ready[i], b + 1)
                for j in range(J):
                    last = nc.vector.tensor_scalar(dst[:, j, :], src[:, j, :], mv[i][:, j, 0:1],
                                                   rstd[i][:, j:j + 1], ALU.subtract, ALU.mult)
                return last

            def front(f, par, slot_):
                first = isinstance(f, int) and f == 0
                if slot_ == 1:
                    dve.wait_ge(x_loaded, 16 * (f + 1))
                    stats(0, cf, f, xin)
                if slot_ == 3:
                    normed(0, f, h0[par], xin).then_inc(h0_ready, 1)
                    dve.wait_ge(h0_ready, f + 1)
                    stats(1, cf, f, h0[par])
                if slot_ == 4:
                    if not first:
                        dve.wait_ge(h1T_ready, KC * f)
                    normed(1, f, h1, h0[par]).then_inc(h1_ready, 1)
                if slot_ in (7, 8):
                    pair = (0, 1) if slot_ == 7 else (2, 3)
                    dve.wait_ge(tap_done, C * f + pair[1] + 1)
                    for s in range(1, TAPS):
                        for c in pair:
                            last = nc.vector.scalar_tensor_tensor(
                                out=acc[:, c, s:L], in0=sq[:, c, 0:L - s],
                                scalar=cw[:, c, TAPS - 1 - s:TAPS - s], in1=acc[:, c, s:L],
                                op0=ALU.mult, op1=ALU.add)
                            if s == TAPS - 1:
                                last.then_inc(conv_done, 1)
                        if s < TAPS - 1:
                            cf.link(f, last)
                if slot_ == 12:
                    dve.wait_ge(proj_ready, f + 1)
                    cf.link(f, nc.vector.tensor_copy(parts[par][:], psG[:]))
                    last = nc.vector.tensor_tensor(rest[64:P], psG[64:P, :], parts[par][64:P], ALU.subtract)
                    cf.link(f, last)
                    nc.vector.tensor_copy(parts[par][64:P], rest[64:P]).then_inc(parts_ready, 1)
                    dve.wait_ge(parts_ready, 2 * f + 1)
                    nc.vector.tensor_tensor(parts[par][96:P], rest[96:P], parts[par][96:P],
                                            ALU.subtract).then_inc(parts_ready, 1)
                if slot_ == 13:
                    dve.wait_ge(soft_ready, f + 1)
                    dve.wait_ge(sq_ready, f + 1)
                    cf.link(f, nc.vector.tensor_tensor(yv[:], yv[:], dt[par][:], ALU.subtract))
                    cf.link(f, nc.vector.scalar_tensor_tensor(out=yv[:], in0=yv[:], scalar=LN_MARGIN, in1=sq[:],
                                                              op0=ALU.add, op1=ALU.min))
                if slot_ == 14:
                    cf.link(f, nc.vector.tensor_tensor(tmp[:], tmp[:], yv[:], ALU.subtract))
                    nc.vector.scalar_tensor_tensor(out=dt[par][:], in0=acc[:], scalar=0.0, in1=tmp[:],
                                                   op0=ALU.max, op1=ALU.add).then_inc(dt_ready, 1)

            def back(b, par, slot_):
                if slot_ == 0:
                    dve.wait_ge(summed, N * (b + 1))
                    for c in range(C):
                        last = nc.vector.scalar_tensor_tensor(out=yv[:, c], in0=xh[par][:, c],
                                                              scalar=dcol[:, c:c + 1], in1=psY[:, c],
                                                              op0=ALU.mult, op1=ALU.add)
                    last.then_inc(yv_done, 1)
                if slot_ == 3:
                    for h in range(2):
                        dve.wait_ge(oproj_ready, 2 * b + h + 1)
                        last = nc.vector.tensor_tensor(ao[:, 2 * h:2 * h + 2].rearrange("p a c -> p (a c)"),
                                                       (psF, psG)[h][:],
                                                       h0[par][:, 2 * h:2 * h + 2].rearrange("p a c -> p (a c)"),
                                                       ALU.add)
                    last.then_inc(ao_done, 1)
                    dve.wait_ge(ao_done, b + 1)
                    stats(2, cb, b, ao)
                if slot_ == 4:
                    dve.wait_ge(xres_loaded, 16 * (b + 1))
                    cb.link(b, normed(2, b, x1, ao))
                    nc.vector.tensor_tensor(x1[:], x1[:], xres[:], ALU.add).then_inc(x1_ready, 1)
                    dve.wait_ge(x1_ready, b + 1)
                    stats(3, cb, b, x1)
                if slot_ == 5:
                    normed(3, b, xn, x1).then_inc(xn_ready, 1)
                if slot_ == 9:
                    dve.wait_ge(logit_ready, b + 1)
                    nc.vector.tensor_copy(logits[:, bass.ds(b * J, J), :].rearrange("p j e -> p (j e)"),
                                          psF[:, 0:J * E]).then_inc(logit_kept, 1)

            def iteration(i, par, do_front, do_back):
                for d in range(N):
                    n = i * N + d
                    dve.wait_ge(decay_ready, n + 1)
                    dve.wait_ge(bx_ready, n + 1)
                    w = st[d % RING]
                    nc.vector.tensor_tensor_scan(w[:].rearrange("p c t -> p (c t)"),
                                                 decay[d % RING][:].rearrange("p c t -> p (c t)"),
                                                 w[:].rearrange("p c t -> p (c t)"),
                                                 0.0, ALU.mult, ALU.add).then_inc(scanned, 1)
                    if do_back:
                        back(i - 1, 1 - par, d)
                    if do_front:
                        front(i + 1, 1 - par, d)
                    dve.wait_ge(c_bcast, n + 1)
                    dve.wait_ge(scanned, n + 1)
                    nc.vector.tensor_tensor(w[:], w[:],
                                            psC[:].unsqueeze(1).broadcast_to([P, C, L]),
                                            ALU.mult).then_inc(weighted, 1)

            for s in range(N):
                front(0, 0, s)
            iteration(0, 0, True, False)
            with dve.Fori(1, NB - 2, 2) as i:
                iteration(i, 1, True, True)
                iteration(i + 1, 0, True, True)
            iteration(NB - 1, 1, False, True)
            for s in range(N):
                back(NB - 1, 1, s)

            rn = [0]

            def link(ins):
                rn[0] += 1
                ins.then_inc(rc, 1)
                dve.wait_ge(rc, rn[0])

            def bt(a):
                return a.unsqueeze(2).broadcast_to([P, NT, E])

            def be(a):
                return a.unsqueeze(1).broadcast_to([P, NT, E])

            oh, cnt, incl, q = rt["oh"], rt["cnt"], rt["incl"], rt["q"]
            dve.wait_ge(iotas, 2)
            dve.wait_ge(logit_kept, NB)
            nc.vector.tensor_copy(iotaJ[:], iotaJi[:])
            link(nc.vector.tensor_copy(iotaE[:], iotaEi[:]))
            nc.vector.tensor_reduce(out=mx[:], in_=logits[:], axis=AX.X, op=ALU.max).then_inc(mx_ready, 1)
            dve.wait_ge(mx_ready, 1)
            link(nc.vector.tensor_tensor(q[:], logits[:], bt(mx[:]), ALU.is_equal))
            link(nc.vector.tensor_tensor(q[:], q[:], be(iotaE[:]), ALU.mult))
            link(nc.vector.tensor_reduce(out=mn[:], in_=q[:], axis=AX.X, op=ALU.min))
            nc.vector.tensor_tensor(oh[:], be(iotaE[:]), bt(mn[:]), ALU.is_equal).then_inc(oh_ready, 1)
            dve.wait_ge(rank_ready, 2)
            link(nc.vector.tensor_copy(cnt[:].rearrange("p t e -> p (t e)"), psC[:, 0:NT * E]))
            for e in range(E):
                last = nc.vector.tensor_tensor_scan(incl[:, :, e], onesT[:], cnt[:, :, e], 0.0, ALU.mult, ALU.add)
            link(last)
            link(nc.vector.tensor_tensor(q[:].rearrange("p t e -> p (t e)"), psB[:, 0:NT * E],
                                         incl[:].rearrange("p t e -> p (t e)"), ALU.add))
            link(nc.vector.tensor_tensor(q[:], q[:], cnt[:], ALU.subtract))
            link(nc.vector.tensor_scalar(ti[:], incl[:, NT - 1, :], float(P - 1), None, ALU.add))
            link(nc.vector.tensor_scalar(ti[:], ti[:], 7, None, ALU.arith_shift_right))
            link(nc.vector.tensor_copy(tf[:], ti[:]))
            link(nc.vector.tensor_tensor_scan(tend[:], onesT[:, 0:E], tf[:], 0.0, ALU.mult, ALU.add))
            link(nc.vector.tensor_tensor(tstart[:], tend[:], tf[:], ALU.subtract))
            link(nc.vector.tensor_scalar(tstart[:], tstart[:], float(P), None, ALU.mult))
            link(nc.vector.tensor_tensor(q[:], q[:], be(tstart[:]), ALU.add))
            link(nc.vector.tensor_tensor(q[:], q[:], oh[:], ALU.mult))
            link(nc.vector.tensor_reduce(out=slotf[:], in_=q[:], axis=AX.X, op=ALU.add))
            nc.vector.tensor_copy(slot[:], slotf[:]).then_inc(slot_ready, 1)
            link(nc.vector.tensor_tensor(le[:], tend[0:1, :].unsqueeze(1).broadcast_to([1, SLOT_TILES, E]),
                                         iotaJ[:].unsqueeze(2).broadcast_to([1, SLOT_TILES, E]), ALU.is_le))
            link(nc.vector.tensor_reduce(out=exf[:], in_=le[:], axis=AX.X, op=ALU.add))
            nc.vector.tensor_scalar(exi[:], exf[:], float(E - 1), None, ALU.min).then_inc(ex_ready, 1)

            def sh_act(g, gp, c):
                u = g * FC + c
                dve.wait_ge(s_silu, u + 1)
                if c == 0 and not (isinstance(g, int) and g < 2):
                    dve.wait_ge(s_down, 2 * (g - 1))
                nc.vector.tensor_tensor(actS[gp][:, c], sg[c % 2][:], psY[:, 2 + c % 2], ALU.mult).then_inc(s_act, 1)

            for g in (0, 1):
                for c in range(FC):
                    sh_act(g, g, c)
            with dve.Fori(2, NB - 1, 2) as g:
                for h in range(2):
                    for c in range(FC):
                        sh_act(g + h, h, c)

            def copy_xsT(s, i):
                dve.wait_ge(xsT_ready, s + 1)
                if not (isinstance(s, int) and s < 2):
                    dve.wait_ge(r_up, s - 1)
                nc.vector.tensor_copy(xsT[i][:].rearrange("p k t -> p (k t)"), psB[:, 0:KC * P]).then_inc(xsT_copied, 1)

            def rt_act(s, i):
                dve.wait_ge(r_silu, s + 1)
                if not (isinstance(s, int) and s < 2):
                    dve.wait_ge(actT_ready, s - 1)
                nc.vector.tensor_tensor(actN[i][:], sg[i][:], psY[:, 2 + i], ALU.mult).then_inc(r_act, 1)

            def copy_actT(s, i):
                dve.wait_ge(actT_ready, s + 1)
                if not (isinstance(s, int) and s < 2):
                    dve.wait_ge(r_down, s - 1)
                nc.vector.tensor_copy(actT[i][:].rearrange("p k t -> p (k t)"), psC[:]).then_inc(actT_copied, 1)

            S = SLOT_TILES
            dve.wait_ge(s_down, 2 * NB)
            copy_xsT(0, 0)
            copy_xsT(1, 1)
            rt_act(0, 0)
            for s in (0, 1):
                copy_xsT(s + 2, s % 2)
                copy_actT(s, s % 2)
                rt_act(s + 1, (s + 1) % 2)
            with dve.Fori(2, S - 4, 2) as s:
                for i in range(2):
                    copy_xsT(s + i + 2, i)
                    copy_actT(s + i, i)
                    rt_act(s + i + 1, 1 - i)
            for s in range(S - 3, S):
                if s + 2 < S:
                    copy_xsT(s + 2, s % 2)
                copy_actT(s, s % 2)
                if s + 1 < S:
                    rt_act(s + 1, (s + 1) % 2)

            def fin_sum(q, i):
                dve.wait_ge(gathered[i], 16 * (q - i) + 32)
                nc.vector.tensor_tensor(fy[i][:], fy[i][:], ysh[:, bass.ds(2 * q, 2), :], ALU.add).then_inc(f_chain, 1)
                dve.wait_ge(f_chain, 2 * q + 1)
                for h in range(2):
                    last = nc.vector.bn_stats(out=fst[i][:, h, :], in_=fy[i][:, h, :])
                last.then_inc(f_chain, 1)
                dve.wait_ge(f_chain, 2 * q + 2)
                nc.vector.memset(carrier[:], 0.0)
                for h in range(2):
                    last = nc.vector.bn_aggr(out=fmv[i][:, h, :], in_=fst[i][:, h, :])
                last.then_inc(f_mv, 1)

            def fin_out(q, i):
                dve.wait_ge(f_rs, 2 * (q + 1))
                dve.wait_ge(f_mv, q + 1)
                for h in range(2):
                    last = nc.vector.tensor_scalar(fy[i][:, h, :], fy[i][:, h, :], fmv[i][:, h, 0:1],
                                                   frs[i][:, h:h + 1], ALU.subtract, ALU.mult)
                last.then_inc(f_normed, 1)
                dve.wait_ge(f_normed, q + 1)
                pair = fx[:, bass.ds(2 * q, 2), :]
                nc.vector.tensor_tensor(pair, fy[i][:], pair, ALU.add).then_inc(f_ready, 1)

            NQ = NT // 2
            fin_sum(0, 0)
            dve.wait_ge(f_loaded[0], 16 * (NB // 2))
            with dve.Fori(0, NQ // 2 - 1, 2) as q:
                for i in range(2):
                    fin_sum(q + i + 1, 1 - i)
                    fin_out(q + i, i)
            dve.wait_ge(f_loaded[1], 16 * (NB // 2))
            with dve.Fori(NQ // 2, NQ - 3, 2) as q:
                for i in range(2):
                    fin_sum(q + i + 1, 1 - i)
                    fin_out(q + i, i)
            fin_sum(NQ - 1, 1)
            fin_out(NQ - 2, 0)
            fin_out(NQ - 1, 1)

        @block.tensor
        def _(pe):
            pe.wait_ge(ident_made, 2)
            pe.wait_ge(consts, 16 * NCONST)
            pe.wait_ge(setup, 1)

            def bcast_row(dst, par, r):
                return nc.tensor.matmul(dst[:], sel[:, r:r + 1].broadcast_to([P, P]), parts[par][:],
                                        start=True, stop=True)

            def front(f, par, slot_):
                first = isinstance(f, int) and f == 0
                if slot_ == 4:
                    pe.wait_ge(h1_ready, f + 1)
                    if not first:
                        pe.wait_ge(z_done, f)
                        pe.wait_ge(parts_ready, 2 * f)
                    if not (isinstance(f, int) and f < 2):
                        pe.wait_ge(ao_done, f - 1)
                    for k in range(KC):
                        for j in range(J):
                            last = nc.tensor.transpose((psF, psG)[k][:, j * P:(j + 1) * P],
                                                       h1[:, j, k * P:(k + 1) * P], ident[:])
                        last.then_inc(h1T_ready, 1)
                if slot_ in (5, 6):
                    pe.wait_ge(hT_ready, f + 1)
                    for c in (0, 1) if slot_ == 5 else (2, 3):
                        if c >= 2:
                            pe.wait_ge(tap_done, C * f + c - 1)
                        for k in range(KC):
                            last = nc.tensor.matmul((psF, psG)[c % 2][:], win[:, k, c * P:(c + 1) * P], hT[:, k],
                                                    start=(k == 0), stop=(k == KC - 1))
                        last.then_inc(inproj_ready, 1)
                if slot_ == 10:
                    pe.wait_ge(xh_ready, f + 1)
                    if not (isinstance(f, int) and f < 2):
                        pe.wait_ge(logit_kept, f - 1)
                    for c in range(C):
                        last = nc.tensor.matmul(psF[:], w_dt[:, c], xh[par][:, c], start=(c == 0), stop=(c == C - 1))
                    last.then_inc(dtin_ready, 1)
                if slot_ == 11:
                    for c in range(C):
                        last = nc.tensor.matmul(psG[:], w_bc[:, c].rearrange("p g r -> p (g r)"), xh[par][:, c],
                                                start=(c == 0), stop=(c == C - 1))
                    last.then_inc(proj_ready, 1)

            def back(b, slot_, fronts):
                if slot_ in (1, 2):
                    pe.wait_ge(ys_ready, b + 1)
                    pe.wait_ge(z_done, fronts)
                    pe.wait_ge(parts_ready, 2 * fronts)
                    if isinstance(b, int) and b == NB - 1:
                        pe.wait_ge(logit_kept, b)
                        pe.wait_ge(xnT_copied, b)
                    h = slot_ - 1
                    for j in (2 * h, 2 * h + 1):
                        for c in range(C):
                            last = nc.tensor.matmul((psF, psG)[h][:, (j % 2) * DIM:(j % 2 + 1) * DIM],
                                                    yv[:, c, j * P:(j + 1) * P], wout[:, c],
                                                    start=(c == 0), stop=(c == C - 1))
                    last.then_inc(oproj_ready, 1)
                if slot_ == 7:
                    pe.wait_ge(xn_ready, b + 1)
                    if isinstance(fronts, int) and fronts == NB:
                        pe.wait_ge(ao_done, b + 1)
                    else:
                        pe.wait_ge(tap_done, C * (fronts + 1))
                    for k in range(KC):
                        for j in range(J):
                            last = nc.tensor.transpose((psF, psG)[k][:, j * P:(j + 1) * P],
                                                       xn[:, j, k * P:(k + 1) * P], ident[:])
                        last.then_inc(xnT_ready, 1)
                if slot_ == 8:
                    pe.wait_ge(xnT_copied, b + 1)
                    for j in range(J):
                        for k in range(KC):
                            last = nc.tensor.matmul(psF[:, j * E:(j + 1) * E], xnTb[:, k, j * P:(j + 1) * P],
                                                    gw[:, k], start=(k == 0), stop=(k == KC - 1))
                    last.then_inc(logit_ready, 1)

            def iteration(i, par, do_front, do_back, last):
                for d in range(N):
                    n = i * N + d
                    pe.wait_ge(weighted, n + 1)
                    if not (last and d == N - 1):
                        bcast_row(psC, par if d < N - 1 else 1 - par, N + (d + 1) % N).then_inc(c_bcast, 1)
                    if do_back:
                        back(i - 1, d, i + 1)
                    if do_front:
                        front(i + 1, 1 - par, d)
                    if d == 0 and do_back:
                        pe.wait_ge(yv_done, i)
                    for c in range(C):
                        s = nc.tensor.matmul(psY[:, c], ident[:], st[d % RING][:, c], start=(d == 0), stop=(d == N - 1))
                    s.then_inc(summed, 1)
                    if not (last and d >= N - 3):
                        if d == N - 3:
                            pe.wait_ge(parts_ready, 2 * (i + 2))
                        pe.wait_ge(b_copied, n + 3)
                        bcast_row(psB, par if d < N - 3 else 1 - par, (d + 3) % N).then_inc(b_bcast, 1)

            for s in range(N):
                front(0, 0, s)
            pe.wait_ge(parts_ready, 2)
            bcast_row(psC, 0, N).then_inc(c_bcast, 1)
            for r in range(3):
                if r > 0:
                    pe.wait_ge(b_copied, r)
                bcast_row(psB, 0, r).then_inc(b_bcast, 1)
            iteration(0, 0, True, False, False)
            with pe.Fori(1, NB - 2, 2) as i:
                iteration(i, 1, True, True, False)
                iteration(i + 1, 0, True, True, False)
            iteration(NB - 1, 1, False, True, True)
            for s in range(N):
                back(NB - 1, s, NB)

            pe.wait_ge(oh_ready, 1)
            oh = rt["oh"][:].rearrange("p t e -> p (t e)")
            nc.tensor.matmul(psB[:, 0:NT * E], upper[:], oh, start=True, stop=True).then_inc(rank_ready, 1)
            nc.tensor.matmul(psC[:, 0:NT * E], ones[:], oh, start=True, stop=True).then_inc(rank_ready, 1)

            def sh_up_(g, c, i):
                u = g * FC + c
                if c == 0:
                    pe.wait_ge(xg_loaded[i], 8 * (g - i) + 16)
                if not (isinstance(u, int) and u < 2):
                    pe.wait_ge(s_act, u - 1)
                for w, bank in ((shg, psY[:, c % 2]), (shu, psY[:, 2 + c % 2])):
                    for k in range(KC):
                        last = nc.tensor.matmul(bank, w[:, k, c * P:(c + 1) * P], xg[i][:, k],
                                                start=(k == 0), stop=(k == KC - 1))
                last.then_inc(s_up, 1)

            def sh_down_(g, gp):
                pe.wait_ge(s_act, (g + 1) * FC)
                for j in range(J):
                    if j % 2 == 0 and not (isinstance(g, int) and g == 0):
                        pe.wait_ge(s_kept, 2 * g + j // 2 - 1)
                    for c in range(FC):
                        last = nc.tensor.matmul((psF, psG)[j // 2][:, (j % 2) * DIM:(j % 2 + 1) * DIM],
                                                actS[gp][:, c, j * P:(j + 1) * P], shd[:, c],
                                                start=(c == 0), stop=(c == FC - 1))
                    if j % 2:
                        last.then_inc(s_down, 1)

            pe.wait_ge(sh_loaded, 48)
            for g in (0, 1):
                for c in range(FC):
                    sh_up_(g, c, g)
            sh_down_(0, 0)
            with pe.Fori(2, NB - 1, 2) as g:
                for h in range(2):
                    for c in range(FC):
                        sh_up_(g + h, c, h)
                    sh_down_(g + h - 1, 1 - h)
            sh_down_(NB - 1, 1)

            def xsT_(s, i):
                pe.wait_ge(xsl_loaded[i], 8 * (s - i) + 16)
                if not (isinstance(s, int) and s == 0):
                    pe.wait_ge(xsT_copied, s)
                for k in range(KC):
                    last = nc.tensor.transpose(psB[:, k * P:(k + 1) * P], xsl[i][:, k * P:(k + 1) * P], ident[:])
                last.then_inc(xsT_ready, 1)

            def up_(s, i):
                pe.wait_ge(xsT_copied, s + 1)
                if not (isinstance(s, int) and s < 2):
                    pe.wait_ge(r_act, s - 1)
                for w, bank in ((wg, psY[:, i]), (wu, psY[:, 2 + i])):
                    for k in range(KC):
                        last = nc.tensor.matmul(bank, xsT[i][:, k], w[:, bass.ds(ereg[i], 1), k].rearrange("p a n -> p (a n)"),
                                                start=(k == 0), stop=(k == KC - 1))
                last.then_inc(r_up, 1)

            def actT_(s, i):
                pe.wait_ge(r_act, s + 1)
                if not (isinstance(s, int) and s == 0):
                    pe.wait_ge(actT_copied, s)
                for c in range(FC):
                    last = nc.tensor.transpose(psC[:, c * P:(c + 1) * P], actN[i][:, c * P:(c + 1) * P], ident[:])
                last.then_inc(actT_ready, 1)

            def down_(s, i):
                pe.wait_ge(actT_copied, s + 1)
                if not (isinstance(s, int) and s < 2):
                    pe.wait_ge(yo_ready, s - 1)
                for c in range(FC):
                    last = nc.tensor.matmul((psF, psG)[i][:, 0:DIM], actT[i][:, c],
                                            wd[:, bass.ds(ereg[i], 1), c].rearrange("p a n -> p (a n)"),
                                            start=(c == 0), stop=(c == FC - 1))
                last.then_inc(r_down, 1)

            S = SLOT_TILES
            ereg = [None, None]

            def expert(s, i):
                ereg[i] = pe.value_load(exi[0:1, bass.ds(s, 1)], min_val=0, max_val=E - 1)

            pe.wait_ge(ex_ready, 1)
            pe.wait_ge(rt_loaded, 16 * 3 * E)
            xsT_(0, 0)
            xsT_(1, 1)
            expert(0, 0)
            up_(0, 0)
            pe.wait_ge(s_kept, 2 * NB)

            def step(s, i, ahead, more):
                if ahead:
                    xsT_(s + 2, i)
                actT_(s, i)
                if more:
                    expert(s + 1, 1 - i)
                    up_(s + 1, 1 - i)
                expert(s, i)
                down_(s, i)

            step(0, 0, True, True)
            step(1, 1, True, True)
            with pe.Fori(2, S - 4, 2) as s:
                step(s, 0, True, True)
                step(s + 1, 1, True, True)
            for s in range(S - 3, S):
                step(s, s % 2, s + 2 < S, s + 1 < S)


def kernel(**inputs):
    import concourse.bacc as _bacc
    from concourse.bass_utils import run_bass_kernel_spmd as _run

    def given(name, transposed=False):
        a = np.asarray(inputs[name])
        return np.ascontiguousarray(a.T if transposed else a)

    def columns(name):
        return np.ascontiguousarray(np.asarray(inputs[name]).reshape(-1, P).T)

    data = {
        "x": given("L0_attn_x"),
        "winT": given("L0_attn_in_proj_w", True),
        "conv_w": given("L0_attn_conv_w"),
        "xprojT": given("L0_attn_x_proj_w", True),
        "dt_w": columns("L0_attn_dt_proj_w"),
        "dt_b": columns("L0_attn_dt_proj_b"),
        "A_log": given("L0_attn_A_log"),
        "D": columns("L0_attn_D"),
        "woutT": given("L0_attn_out_proj_w", True),
        "norm_w": columns("L0_attn_norm_w"),
        "norm_b": columns("L0_attn_norm_b"),
        "gate_w": given("L0_ffn_gate_w"),
        "sh_gate": given("L0_ffn_sh_gate"),
        "sh_up": given("L0_ffn_sh_up"),
        "sh_down": given("L0_ffn_sh_down"),
        "rt_gate": given("L0_ffn_rt_gate"),
        "rt_up": given("L0_ffn_rt_up"),
        "rt_down": given("L0_ffn_rt_down"),
    }
    nc = _bacc.Bacc("TRN2", target_bir_lowering=False, num_devices=1)
    args = [nc.dram_tensor(f"in_{n}", a.shape, mybir.dt.from_np(a.dtype), kind="ExternalInput").ap()
            for n, a in data.items()]
    res = nc.dram_tensor("result", data["x"].shape, F32, kind="ExternalOutput").ap()
    build(nc, *args, res)
    r = _run(nc, [{f"in_{n}": a for n, a in data.items()}], core_ids=[0])
    return r.results[0]["result"]
```

```python
from contextlib import ExitStack

import numpy as np
import concourse.bass as bass
from concourse import mybir
from concourse.alu_op_type import AluOpType as ALU

F32 = mybir.dt.float32
BF16 = mybir.dt.bfloat16
I32 = mybir.dt.int32
U32 = mybir.dt.uint32
ACT = mybir.ActivationFunctionType
AX = mybir.AxisListType
P = 128
EPS = 1e-5
HALF_ROOT = float(np.sqrt(0.5))
LN_MARGIN = 2e-9


def build(nc, x, winT, conv_w, xprojT, dt_w, dt_b, A_log, D, woutT, norm_w, norm_b,
          gate_w, sh_gate, sh_up, sh_down, rt_gate, rt_up, rt_down, out):
    NB, L, DIM = x.shape
    DIN = winT.shape[1]
    N = A_log.shape[1]
    TAPS = conv_w.shape[1]
    KC = DIM // P
    C = DIN // P
    J = L // P
    NT = NB * J
    TOK = NB * L
    E, _, FF = rt_gate.shape
    FC = FF // P
    SLOT_TILES = (TOK + E * (P - 1)) // P
    CL = C * L
    RING = 4
    FRING = 8
    G3 = 2 * N

    x1_d = nc.dram_tensor("x1_rows", (TOK, DIM), F32).ap()
    xn_d = nc.dram_tensor("xn_rows", (TOK, DIM), F32).ap()
    xnT_d = nc.dram_tensor("xn_columns", (NB, P, KC * L), F32).ap()
    xs_d = nc.dram_tensor("slot_in", (SLOT_TILES * P, DIM), F32).ap()
    y_d = nc.dram_tensor("slot_out", (SLOT_TILES * P, DIM), F32).ap()

    ctx = ExitStack()
    with ctx:
        def sb(name, shape, dt=F32, where=ctx):
            return where.enter_context(nc.sbuf_tensor(name, shape, dt))

        def sem(name):
            return ctx.enter_context(nc.semaphore(name))

        ps = [ctx.enter_context(nc.psum_tensor(f"bank{i}", [P, 512], F32)) for i in range(4, 8)]
        psY = ctx.enter_context(nc.psum_tensor("psY", [P, C, L], F32))
        psB, psC, psF, psG = ps

        ident = sb("ident", [P, P])
        logits = sb("logits", [P, NT, E])
        epsc = sb("epsc", [P, 1])
        mone = sb("mone", [P, 1])
        zrow = sb("zrow", [P, DIM])
        carrier = sb("carrier", [P, 1])

        A = ExitStack()
        ctx.enter_context(A)
        win = sb("win", [P, KC, DIN], where=A)
        cw = sb("cw", [P, C, TAPS], where=A)
        xp = sb("xp", [P, C, 1 + G3], where=A)
        w_dt = sb("w_dt", [P, C, P], where=A)
        w_bc = sb("w_bc", [P, C, 4, G3], where=A)
        dtw = sb("dtw", [P, C], where=A)
        dtb = sb("dtb", [P, C], where=A)
        alog = sb("alog", [P, C, N], where=A)
        aneg = sb("aneg", [P, C, N], where=A)
        dcol = sb("dcol", [P, C], where=A)
        wout = sb("wout", [P, C, DIM], where=A)
        nw = sb("nw", [P, KC], where=A)
        nb_ = sb("nb", [P, KC], where=A)
        gw = sb("gw", [P, KC, E], where=A)
        sel_f = sb("sel_f", [P, G3], where=A)
        sel = sb("sel", [P, G3], BF16, where=A)
        decay = [sb(f"decay{i}", [P, C, L], where=A) for i in range(RING)]
        st = [sb(f"state{i}", [P, C, L], where=A) for i in range(RING)]
        dt = [sb(f"dt{i}", [P, C, L], where=A) for i in range(2)]
        xh = [sb(f"xh{i}", [P, C, L], where=A) for i in range(2)]
        acc = sb("acc", [P, C, L], where=A)
        tmp = sb("tmp", [P, C, L], where=A)
        yv = sb("yv", [P, C, L], where=A)
        sq = sb("sq", [P, C, L], where=A)
        bbc = [sb(f"bbc{i}", [P, L], where=A) for i in range(RING)]
        parts = [sb(f"parts{i}", [P, L], BF16, where=A) for i in range(2)]
        rest = sb("rest", [P, L], where=A)
        xin = sb("xin", [P, J, DIM], where=A)
        xres = sb("xres", [P, J, DIM], where=A)
        h0 = [sb(f"h0_{i}", [P, J, DIM], where=A) for i in range(2)]
        h1 = sb("h1", [P, J, DIM], where=A)
        hT = sb("hT", [P, KC, L], where=A)
        ao = sb("ao", [P, J, DIM], where=A)
        x1 = sb("x1", [P, J, DIM], where=A)
        xn = sb("xn", [P, J, DIM], where=A)
        xnTb = sb("xnTb", [P, KC, L], where=A)
        bst = [sb(f"bst{i}", [P, J, 6], where=A) for i in range(4)]
        mv = [sb(f"mv{i}", [P, J, 2], where=A) for i in range(4)]
        lnv = [sb(f"lnv{i}", [P, J], where=A) for i in range(4)]
        rstd = [sb(f"rstd{i}", [P, J], where=A) for i in range(4)]
        nmr = [sb(f"nmr{i}", [P, J], where=A) for i in range(4)]
        A.close()

        M = ctx.enter_context(ExitStack())
        WG = ExitStack()
        ctx.enter_context(WG)
        wg = sb("wg", [P, E, KC, FF], where=WG)
        WG.close()
        HALF = NT // 2
        fx1 = sb("fx1", [P, HALF, DIM], where=M)
        sb("wg_rest", [P, E * KC * FF - HALF * DIM], where=M)
        wu = sb("wu", [P, E, KC, FF], where=M)
        wd = sb("wd", [P, E, FC, DIM], where=M)
        SH = ExitStack()
        ctx.enter_context(SH)
        shg = sb("shg", [P, KC, FF], where=SH)
        shu = sb("shu", [P, KC, FF], where=SH)
        shd = sb("shd", [P, FC, DIM], where=SH)
        xg = [sb("xg0", [P, KC, L], where=SH)]
        SH.close()
        fx0 = sb("fx0", [P, HALF, DIM], where=M)
        ysh = sb("ysh", [P, NT, DIM], where=M)
        sg = [sb(f"sg{i}", [P, FF], where=M) for i in range(2)]
        xg.append(sb("xg1", [P, KC, L], where=M))
        xsl = [sb(f"xsl{i}", [P, DIM], where=M) for i in range(2)]
        xsT = [sb(f"xsT{i}", [P, KC, P], where=M) for i in range(2)]
        MS = ExitStack()
        ctx.enter_context(MS)
        actS = [sb(f"actS{i}", [P, FC, L], where=MS) for i in range(2)]
        MS.close()
        actN = [sb(f"actN{i}", [P, FF], where=M) for i in range(2)]
        actT = [sb(f"actT{i}", [P, FC, P], where=M) for i in range(2)]
        yo = [sb(f"yo{i}", [P, DIM], where=M) for i in range(2)]
        fy = [sb(f"fy{i}", [P, 2, DIM], where=M) for i in range(FRING)]
        R = ctx.enter_context(ExitStack())
        rt = {n: sb(n, [P, NT, E], where=R) for n in ("oh", "cnt", "incl", "q")}
        iotaE = sb("iotaE", [P, E], where=R)
        iotaEi = sb("iotaEi", [P, E], I32, where=R)
        iotaJ = sb("iotaJ", [1, SLOT_TILES], where=R)
        iotaJi = sb("iotaJi", [1, SLOT_TILES], I32, where=R)
        mx = sb("mx", [P, NT], where=R)
        mn = sb("mn", [P, NT], where=R)
        score = sb("score", [P, NT], where=R)
        slotf = sb("slotf", [P, NT], where=R)
        slot = sb("slot", [P, NT], I32, where=R)
        ti = sb("ti", [P, E], I32, where=R)
        tf = sb("tf", [P, E], where=R)
        tend = sb("tend", [P, E], where=R)
        tstart = sb("tstart", [P, E], where=R)
        onesT = sb("onesT", [P, NT], where=R)
        upper = sb("upper", [P, P], where=R)
        ones = sb("ones", [P, P], where=R)
        le = sb("le", [1, SLOT_TILES, E], where=R)
        exf = sb("exf", [1, SLOT_TILES], where=R)
        exi = sb("exi", [1, SLOT_TILES], I32, where=R)
        xrow = [sb(f"xrow{i}", [P, J, DIM], where=R) for i in range(2)]
        fst = [sb(f"fst{i}", [P, 2, 6], where=R) for i in range(FRING)]
        fmv = [sb(f"fmv{i}", [P, 2, 2], where=R) for i in range(FRING)]
        fln = [sb(f"fln{i}", [P, 2], where=R) for i in range(FRING)]
        fnm = [sb(f"fnm{i}", [P, 2], where=R) for i in range(FRING)]
        frs = [sb(f"frs{i}", [P, 2], where=R) for i in range(FRING)]

        consts = sem("consts_loaded")
        slots_zeroed = sem("slots_zeroed")
        ident_made = sem("ident_made")
        setup = sem("setup")
        aexp = sem("aexp")
        zeroed = sem("zeroed")
        x_loaded = sem("x_loaded")
        xres_loaded = sem("xres_loaded")
        b_bcast = sem("b_bcast")
        c_bcast = sem("c_bcast")
        b_copied = sem("b_copied")
        decay_ready = sem("decay_ready")
        bx_ready = sem("bx_ready")
        scanned = sem("scanned")
        weighted = sem("weighted")
        summed = sem("summed")
        vf = sem("vector_front_chain")
        vb = sem("vector_back_chain")
        sf = sem("scalar_chain")
        mv_ready = [sem(f"mv_ready{i}") for i in range(4)]
        rs_ready = [sem(f"rs_ready{i}") for i in range(4)]
        h0_ready = sem("h0_ready")
        h1_ready = sem("h1_ready")
        h1T_ready = sem("h1T_ready")
        hT_ready = sem("hT_ready")
        inproj_ready = sem("inproj_ready")
        tap_done = sem("tap_done")
        conv_done = sem("conv_done")
        xh_ready = sem("xh_ready")
        dtin_ready = sem("dtin_ready")
        proj_ready = sem("proj_ready")
        z_done = sem("z_done")
        sq_ready = sem("sq_ready")
        soft_ready = sem("soft_ready")
        loss_ready = sem("loss_ready")
        parts_ready = sem("parts_ready")
        dt_ready = sem("dt_ready")
        yv_done = sem("yv_done")
        ys_ready = sem("ys_ready")
        oproj_ready = sem("oproj_ready")
        ao_done = sem("ao_done")
        x1_normed = sem("x1_normed")
        x1_ready = sem("x1_ready")
        xn_ready = sem("xn_ready")
        xnT_ready = sem("xnT_ready")
        xnT_copied = sem("xnT_copied")
        logit_ready = sem("logit_ready")
        logit_kept = sem("logit_kept")
        x1_stored = sem("x1_stored")
        xn_stored = sem("xn_stored")
        xnT_kept = sem("xnT_kept")
        sh_loaded = sem("shared_weights_loaded")
        rt_loaded = sem("routed_weights_loaded")
        iotas = sem("iotas")
        rc = sem("routing_chain")
        oh_ready = sem("oh_ready")
        rank_ready = sem("rank_ready")
        mx_ready = sem("mx_ready")
        score_ready = sem("score_ready")
        slot_ready = sem("slot_ready")
        ex_ready = sem("ex_ready")
        xrow_loaded = [sem(f"xrow_loaded{i}") for i in range(2)]
        xrow_scaled = sem("xrow_scaled")
        scattered = [sem(f"scattered{i}") for i in range(2)]
        xg_loaded = [sem(f"xg_loaded{i}") for i in range(2)]
        s_up = sem("shared_up_ready")
        s_silu = sem("shared_silu")
        s_act = sem("shared_act")
        s_down = sem("shared_down_ready")
        s_kept = sem("shared_kept")
        xsl_loaded = [sem(f"xsl_loaded{i}") for i in range(2)]
        xsT_ready = sem("xsT_ready")
        xsT_copied = sem("xsT_copied")
        r_up = sem("routed_up_ready")
        r_silu = sem("routed_silu")
        r_act = sem("routed_act")
        actT_ready = sem("actT_ready")
        actT_copied = sem("actT_copied")
        r_down = sem("routed_down_ready")
        yo_ready = sem("yo_ready")
        yo_stored = [sem(f"yo_stored{i}") for i in range(2)]
        gathered = [sem(f"gathered{i}") for i in range(FRING)]
        f_loaded = [sem(f"f_half_loaded{i}") for i in range(2)]
        f_chain = sem("final_chain")
        f_normed = sem("final_normed")
        f_mv = sem("final_mv")
        f_rs = sem("final_rs")
        f_ready = sem("final_ready")
        f_stored = [sem(f"f_stored{i}") for i in range(2)]

        NCONST = 11
        xb_v = x.rearrange("b (j p) c -> b p j c", p=P)
        x1b_v = x1_d.rearrange("(b j p) c -> b p j c", p=P, j=J)
        xnb_v = xn_d.rearrange("(b j p) c -> b p j c", p=P, j=J)
        x1t_v = x1_d.rearrange("(t p) c -> p t c", p=P)
        xst_v = xs_d.rearrange("(t p) c -> t p c", p=P)
        yt_v = y_d.rearrange("(t p) c -> t p c", p=P)
        outp_v = out.rearrange("b (q h p) c -> (b q) p h c", p=P, h=2)

        def pick(v, i):
            return v[bass.ds(i, 1)].rearrange("a p c -> p (a c)") if len(v.shape) == 3 else \
                v[bass.ds(i, 1)].rearrange("a p j c -> p (a j) c")

        block = ctx.enter_context(nc.Block())

        @block.sync
        def _(sp):
            sp.dma_start(xin[:], xb_v[0]).then_inc(x_loaded, 16)
            for dst, src in (
                (win, winT.rearrange("(k p) n -> p k n", p=P)),
                (cw, conv_w.rearrange("(c p) k -> p c k", p=P)),
                (xp, xprojT.rearrange("(c p) r -> p c r", p=P)),
                (dtw, dt_w),
                (dtb, dt_b),
                (alog, A_log.rearrange("(c p) d -> p c d", p=P)),
                (dcol, D),
                (nw, norm_w),
                (nb_, norm_b),
                (gw, gate_w.rearrange("(k p) e -> p k e", p=P)),
                (wout, woutT.rearrange("(c p) n -> p c n", p=P)),
            ):
                sp.dma_start(dst[:], src).then_inc(consts, 16)
            sp.wait_ge(zeroed, 1)
            sp.dma_start(xs_d.rearrange("(t p) c -> p t c", p=P),
                         zrow[:].unsqueeze(1).broadcast_to([P, SLOT_TILES, DIM])).then_inc(slots_zeroed, 16)

            def back_dma(b):
                if not (isinstance(b, int) and b == 0):
                    sp.wait_ge(x1_stored, 16 * b)
                    sp.wait_ge(xn_stored, 16 * b)
                    sp.wait_ge(xnT_kept, 16 * b)
                    sp.wait_ge(x1_ready, b)
                sp.dma_start(xres[:], pick(xb_v, b)).then_inc(xres_loaded, 16)
                sp.wait_ge(x1_ready, b + 1)
                sp.dma_start(pick(x1b_v, b), x1[:]).then_inc(x1_stored, 16)
                sp.wait_ge(xn_ready, b + 1)
                sp.dma_start(pick(xnb_v, b), xn[:]).then_inc(xn_stored, 16)
                sp.wait_ge(xnT_copied, b + 1)
                sp.dma_start(xnT_d[bass.ds(b, 1)].rearrange("a p c -> p (a c)"),
                             xnTb[:].rearrange("p k t -> p (k t)")).then_inc(xnT_kept, 16)

            def next_x(f):
                sp.wait_ge(h0_ready, f)
                sp.dma_start(xin[:], pick(xb_v, f)).then_inc(x_loaded, 16)

            next_x(1)
            next_x(2)
            back_dma(0)
            with sp.Fori(1, NB - 2) as b:
                next_x(b + 2)
                back_dma(b)
            back_dma(NB - 2)
            back_dma(NB - 1)

            sp.wait_ge(xnT_kept, 16 * NB)
            sp.wait_ge(x1_stored, 16 * NB)
            sp.wait_ge(xn_stored, 16 * NB)
            sp.wait_ge(logit_kept, NB)
            sp.dma_start(xg[1][:].rearrange("p k t -> p (k t)"), xnT_d[1]).then_inc(xg_loaded[1], 16)
            for i in range(2):
                sp.dma_start(xrow[i][:], xnb_v[i]).then_inc(xrow_loaded[i], 16)
            for e in range(E):
                sp.dma_start(wg[:, e], rt_gate[e].rearrange("(k p) n -> p k n", p=P)).then_inc(rt_loaded, 16)
                sp.dma_start(wu[:, e], rt_up[e].rearrange("(k p) n -> p k n", p=P)).then_inc(rt_loaded, 16)
                sp.dma_start(wd[:, e], rt_down[e].rearrange("(k p) n -> p k n", p=P)).then_inc(rt_loaded, 16)

            for b in range(2, NB):
                sp.wait_ge(scattered[b % 2], 16 * J * (b // 2))
                sp.dma_start(xrow[b % 2][:], xnb_v[b]).then_inc(xrow_loaded[b % 2], 16)

            sp.wait_ge(scattered[0], 16 * (NT // 2))
            sp.wait_ge(scattered[1], 16 * (NT // 2))

            def load_slots(s, i):
                sp.dma_start(xsl[i][:], pick(xst_v, s)).then_inc(xsl_loaded[i], 16)

            load_slots(0, 0)
            load_slots(1, 1)
            def load_residual(dst, h):
                for g in range(NB // 2):
                    rows = slice((h * NB // 2 + g) * J, (h * NB // 2 + g + 1) * J)
                    sp.dma_start(dst[:, g * J:(g + 1) * J, :], x1t_v[:, rows, :]).then_inc(f_loaded[h], 16)

            sp.wait_ge(s_down, 2 * NB)
            load_residual(fx0, 0)
            with sp.Fori(0, SLOT_TILES - 4, 2) as s:
                for i in range(2):
                    sp.wait_ge(xsT_ready, s + i + 1)
                    load_slots(s + i + 2, i)
            for s in range(SLOT_TILES - 3, SLOT_TILES - 2):
                sp.wait_ge(xsT_ready, s + 1)
                load_slots(s + 2, s % 2)

            sp.wait_ge(r_up, SLOT_TILES)
            load_residual(fx1, 1)

            def store_out(q, i, src, first):
                sp.wait_ge(f_ready, q + 1)
                sp.dma_start(outp_v[bass.ds(q, 1)].rearrange("a p h c -> p (a h) c"),
                             src[:, bass.ds(2 * (q - first), 2), :]).then_inc(f_stored[i], 16)

            NQ = NT // 2
            for h, src in enumerate((fx0, fx1)):
                with sp.Fori(h * NQ // 2, (h + 1) * NQ // 2 - 1, 2) as q:
                    for i in range(2):
                        store_out(q + i, i, src, h * NQ // 2)
            sp.wait_ge(f_stored[0], 16 * (NQ // 2))
            sp.wait_ge(f_stored[1], 16 * (NQ // 2))

        @block.gpsimd
        def _(pool):
            nc.gpsimd.memset(zrow[:], 0.0).then_inc(zeroed, 1)
            nc.gpsimd.memset(ident[:], 0.0).then_inc(ident_made, 1)
            pool.wait_ge(ident_made, 1)
            nc.gpsimd.affine_select(out=ident[:], in_=ident[:], compare_op=ALU.not_equal, fill=1.0, base=0,
                                    pattern=[[-1, P]], channel_multiplier=1).then_inc(ident_made, 1)

            def input_step(b, par, d):
                n = b * N + d
                if d == 0:
                    pool.wait_ge(xh_ready, b + 1)
                pool.wait_ge(b_copied, n + 1)
                if not (isinstance(n, int) and n < RING):
                    pool.wait_ge(summed, n - RING + 1)
                nc.gpsimd.tensor_tensor(st[d % RING][:], xh[par][:],
                                        bbc[d % RING][:].unsqueeze(1).broadcast_to([P, C, L]),
                                        ALU.mult).then_inc(bx_ready, 1)

            def loss(f, par):
                pool.wait_ge(soft_ready, f + 1)
                nc.gpsimd.tensor_tensor(yv[:], yv[:], dt[par][:], ALU.subtract).then_inc(loss_ready, 1)

            def front_loss(i, par, d):
                if d == N - 2:
                    loss(i + 1, 1 - par)

            loss(0, 0)
            for d in range(N):
                input_step(0, 0, d)
                front_loss(0, 0, d)
            with pool.Fori(1, NB - 2, 2) as b:
                for q in range(2):
                    for d in range(N):
                        input_step(b + q, (1 + q) % 2, d)
                        front_loss(b + q, (1 + q) % 2, d)
            for d in range(N):
                input_step(NB - 1, 1, d)

            pool.wait_ge(xnT_kept, 16 * NB)
            pool.wait_ge(logit_kept, NB)
            pool.wait_ge(x1_stored, 16 * NB)
            pool.wait_ge(xn_stored, 16 * NB)
            nc.gpsimd.iota(iotaEi[:], pattern=[[1, E]], base=-E, channel_multiplier=0)
            nc.gpsimd.iota(iotaJi[:], pattern=[[1, SLOT_TILES]], base=0, channel_multiplier=0)
            nc.gpsimd.memset(ones[:], 1.0)
            nc.gpsimd.memset(onesT[:], 1.0)
            nc.gpsimd.memset(upper[:], 1.0).then_inc(iotas, 1)
            pool.wait_ge(iotas, 1)
            nc.gpsimd.affine_select(out=upper[:], in_=upper[:], compare_op=ALU.is_gt, fill=0.0, base=0,
                                    pattern=[[1, P]], channel_multiplier=-1).then_inc(iotas, 1)

            pool.wait_ge(score_ready, 1)
            pool.wait_ge(slot_ready, 1)
            pool.wait_ge(slots_zeroed, 16)
            for b in range(NB):
                pool.wait_ge(xrow_loaded[b % 2], 16 * (b // 2 + 1))
                nc.gpsimd.tensor_tensor(xrow[b % 2][:], xrow[b % 2][:],
                                        score[:, b * J:(b + 1) * J].unsqueeze(2).broadcast_to([P, J, DIM]),
                                        ALU.mult).then_inc(xrow_scaled, 1)
                pool.wait_ge(xrow_scaled, b + 1)
                for j in range(J):
                    t = b * J + j
                    nc.gpsimd.indirect_dma_start(
                        out=xs_d, out_offset=bass.IndirectOffsetOnAxis(slot[:, t:t + 1].bitcast(U32), 0),
                        in_=xrow[b % 2][:, j, :], in_offset=None).then_inc(scattered[b % 2], 16)

            pool.wait_ge(yo_stored[0], 16 * ((SLOT_TILES + 1) // 2))
            pool.wait_ge(yo_stored[1], 16 * (SLOT_TILES // 2))
            for t in range(NT):
                q = t // 2
                if t % 2 == 0 and q >= FRING:
                    pool.wait_ge(f_ready, q - FRING + 1)
                nc.gpsimd.indirect_dma_start(
                    out=fy[q % FRING][:, t % 2, :], out_offset=None, in_=y_d,
                    in_offset=bass.IndirectOffsetOnAxis(slot[:, t:t + 1].bitcast(U32), 0),
                ).then_inc(gathered[q % FRING], 16)


        @block.scalar
        def _(act):
            def ln_exp_tables():
                nc.scalar.preload_act_table_set("natural_log_exp_and_others")

            ln_exp_tables()
            act.wait_ge(consts, 16 * NCONST)
            nc.scalar.activation(alog[:], alog[:], ACT.Exp).then_inc(aexp, 1)
            act.wait_ge(setup, 1)

            def inv_std(i, b):
                act.wait_ge(mv_ready[i], b + 1)
                nc.scalar.activation(lnv[i][:], mv[i][:, :, 1], ACT.Ln, bias=epsc[:]).then_inc(rs_ready[i], 1)
                act.wait_ge(rs_ready[i], 2 * b + 1)
                nc.scalar.activation(rstd[i][:], lnv[i][:], ACT.Exp, scale=-0.5).then_inc(rs_ready[i], 1)

            def normed(i, b, dst, src):
                act.wait_ge(mv_ready[i], b + 1)
                nc.scalar.activation(lnv[i][:], mv[i][:, :, 1], ACT.Ln, bias=epsc[:])
                nc.scalar.activation(nmr[i][:], mv[i][:, :, 0], ACT.Identity, scale=-1.0).then_inc(rs_ready[i], 1)
                act.wait_ge(rs_ready[i], 3 * b + 1)
                nc.scalar.activation(rstd[i][:], lnv[i][:], ACT.Exp, scale=-0.5).then_inc(rs_ready[i], 1)
                act.wait_ge(rs_ready[i], 3 * b + 2)
                for j in range(J):
                    last = nc.scalar.activation(nmr[i][:, j:j + 1], nmr[i][:, j:j + 1], ACT.Identity,
                                                scale=rstd[i][:, j:j + 1])
                last.then_inc(rs_ready[i], 1)
                act.wait_ge(rs_ready[i], 3 * b + 3)
                for j in range(J):
                    last = nc.scalar.activation(dst[:, j, :], src[:, j, :], ACT.Identity,
                                                scale=rstd[i][:, j:j + 1], bias=nmr[i][:, j:j + 1])
                return last

            def front(f, par, slot_):
                first = isinstance(f, int) and f == 0
                if slot_ == 2:
                    inv_std(0, f)
                if slot_ == 4:
                    if not first:
                        act.wait_ge(h1T_ready, KC * f)
                    normed(1, f, h1, h0[par]).then_inc(h1_ready, 1)
                if slot_ == 5:
                    for k in range(KC):
                        act.wait_ge(h1T_ready, KC * f + k + 1)
                        if k == 0 and not first:
                            act.wait_ge(inproj_ready, C * f)
                        last = nc.scalar.activation(hT[:, k], (psF, psG)[k][:], ACT.Identity,
                                                    scale=nw[:, k:k + 1], bias=nb_[:, k:k + 1])
                    last.then_inc(hT_ready, 1)
                if slot_ in (6, 7):
                    for c in (0, 1) if slot_ == 6 else (2, 3):
                        act.wait_ge(inproj_ready, C * f + c + 1)
                        if c == 0 and not first:
                            act.wait_ge(dt_ready, f)
                        nc.scalar.activation(acc[:, c], (psF, psG)[c % 2][:], ACT.Identity,
                                             scale=cw[:, c, TAPS - 1:TAPS])
                        nc.scalar.activation(sq[:, c], (psF, psG)[c % 2][:], ACT.Identity).then_inc(tap_done, 1)
                if slot_ == 9:
                    act.wait_ge(conv_done, C * (f + 1))
                    if not (isinstance(f, int) and f < 2):
                        act.wait_ge(yv_done, f - 1)
                    nc.scalar.activation(xh[par][:], acc[:], ACT.Silu).then_inc(xh_ready, 1)
                    ln_exp_tables()
                if slot_ == 10:
                    act.wait_ge(dtin_ready, f + 1)
                    act.wait_ge(xh_ready, f + 1)
                    for c in range(C):
                        last = nc.scalar.activation(acc[:, c], psF[:], ACT.Identity,
                                                    scale=dtw[:, c:c + 1], bias=dtb[:, c:c + 1])
                    last.then_inc(z_done, 1)
                    act.wait_ge(z_done, f + 1)
                    nc.scalar.activation(tmp[:], acc[:], ACT.Abs).then_inc(sf, 1)
                if slot_ == 11:
                    act.wait_ge(sf, 4 * f + 1)
                    nc.scalar.activation(tmp[:], tmp[:], ACT.Exp, scale=-1.0).then_inc(sf, 1)
                if slot_ == 12:
                    act.wait_ge(sf, 4 * f + 2)
                    if not (isinstance(f, int) and f < 2):
                        act.wait_ge(oproj_ready, 2 * f - 2)
                    nc.scalar.activation(yv[:], tmp[:], ACT.Identity, bias=1.0).then_inc(sf, 1)
                    act.wait_ge(sf, 4 * f + 3)
                    nc.scalar.activation(yv[:], yv[:], ACT.Identity, bias=mone[:]).then_inc(sf, 1)
                    act.wait_ge(sf, 4 * f + 4)
                    nc.scalar.activation(dt[par][:], yv[:], ACT.Ln, bias=1.0).then_inc(soft_ready, 1)
                    nc.scalar.activation(sq[:], tmp[:], ACT.Square, scale=HALF_ROOT).then_inc(sq_ready, 1)

            def back(b, slot_):
                if slot_ == 1:
                    act.wait_ge(yv_done, b + 1)
                    nc.scalar.activation(yv[:], yv[:], ACT.Silu).then_inc(ys_ready, 1)
                    ln_exp_tables()
                if slot_ == 8:
                    act.wait_ge(xres_loaded, 16 * (b + 1))
                    normed(2, b, x1, ao).then_inc(x1_normed, 1)
                if slot_ == 13:
                    normed(3, b, xn, x1).then_inc(xn_ready, 1)
                if slot_ == 14:
                    for k in range(KC):
                        act.wait_ge(xnT_ready, KC * b + k + 1)
                        last = nc.scalar.activation(xnTb[:, k], (psF, psG)[k][:], ACT.Identity)
                    last.then_inc(xnT_copied, 1)

            def copy_b(n, r):
                act.wait_ge(b_bcast, n + 1)
                if not (isinstance(n, int) and n < RING):
                    act.wait_ge(bx_ready, n - RING + 1)
                nc.scalar.activation(bbc[r][:], psB[:], ACT.Identity).then_inc(b_copied, 1)

            def decays(n, par, d):
                if not (isinstance(n, int) and n < RING):
                    act.wait_ge(scanned, n - RING + 1)
                for c in range(C):
                    e = nc.scalar.activation(decay[d % RING][:, c, 1:L], dt[par][:, c, 1:L], ACT.Exp,
                                             scale=aneg[:, c, d:d + 1])
                e.then_inc(decay_ready, 1)

            def iteration(i, par, do_front, do_back, last):
                for d in range(N):
                    n = i * N + d
                    if d == N - 1 and not last:
                        act.wait_ge(dt_ready, i + 2)
                    if not (last and d == N - 1):
                        decays(n + 1, par if d < N - 1 else 1 - par, (d + 1) % N)
                    if not (last and d >= N - 2):
                        copy_b(n + 2, (d + 2) % RING)
                    if do_back:
                        back(i - 1, d)
                    if do_front:
                        front(i + 1, 1 - par, d)

            for s in range(N):
                front(0, 0, s)
            copy_b(0, 0)
            copy_b(1, 1)
            act.wait_ge(dt_ready, 1)
            decays(0, 0, 0)
            iteration(0, 0, True, False, False)
            with act.Fori(1, NB - 2, 2) as i:
                iteration(i, 1, True, True, False)
                iteration(i + 1, 0, True, True, False)
            iteration(NB - 1, 1, False, True, True)
            for s in range(2):
                back(NB - 1, s)
            for dst, src in ((shg, sh_gate), (shu, sh_up), (shd, sh_down)):
                act.dma_start(dst[:], src.rearrange("(k p) n -> p k n", p=P)).then_inc(sh_loaded, 16)
            act.wait_ge(xnT_kept, 16 * (NB - 1))
            act.dma_start(xg[0][:].rearrange("p k t -> p (k t)"), xnT_d[0]).then_inc(xg_loaded[0], 16)
            for s in range(2, N):
                back(NB - 1, s)

            act.wait_ge(mx_ready, 1)
            nc.scalar.activation(score[:], mx[:], ACT.Sigmoid).then_inc(score_ready, 1)

            def sh_silu(g, c):
                u = g * FC + c
                act.wait_ge(s_up, u + 1)
                if not (isinstance(u, int) and u < 2):
                    act.wait_ge(s_act, u - 1)
                nc.scalar.activation(sg[c % 2][:], psY[:, c % 2], ACT.Silu).then_inc(s_silu, 1)

            def sh_keep(g):
                for h in range(2):
                    act.wait_ge(s_down, 2 * g + h + 1)
                    nc.scalar.activation(ysh[:, bass.ds(g * J + 2 * h, 2), :].rearrange("p a c -> p (a c)"),
                                         (psF, psG)[h][:], ACT.Identity).then_inc(s_kept, 1)

            for c in range(FC):
                sh_silu(0, c)
            def load_group(g, i):
                act.wait_ge(s_up, (g - 1) * FC)
                act.dma_start(xg[i][:].rearrange("p k t -> p (k t)"),
                              xnT_d[bass.ds(g, 1)].rearrange("a p c -> p (a c)")).then_inc(xg_loaded[i], 16)

            load_group(2, 0)
            for c in range(FC):
                sh_silu(1, c)
            load_group(3, 1)
            sh_keep(0)
            with act.Fori(2, NB - 3, 2) as g:
                for h in range(2):
                    for c in range(FC):
                        sh_silu(g + h, c)
                    load_group(g + h + 2, h)
                    sh_keep(g + h - 1)
            for g in (NB - 2, NB - 1):
                for c in range(FC):
                    sh_silu(g, c)
                sh_keep(g - 1)
            sh_keep(NB - 1)

            def rt_silu(s, i):
                act.wait_ge(r_up, s + 1)
                if not (isinstance(s, int) and s < 2):
                    act.wait_ge(r_act, s - 1)
                nc.scalar.activation(sg[i][:], psY[:, i], ACT.Silu).then_inc(r_silu, 1)

            def rt_out(s, i):
                act.wait_ge(r_down, s + 1)
                if not (isinstance(s, int) and s < 2):
                    act.wait_ge(yo_stored[i], (s - i) * 8)
                nc.scalar.activation(yo[i][:], (psF, psG)[i][:, 0:DIM], ACT.Identity).then_inc(yo_ready, 1)
                act.wait_ge(yo_ready, s + 1)
                act.dma_start(pick(yt_v, s), yo[i][:]).then_inc(yo_stored[i], 16)

            act.wait_ge(s_kept, 2 * NB)
            rt_silu(0, 0)
            rt_silu(1, 1)
            rt_out(0, 0)
            rt_silu(2, 0)
            rt_out(1, 1)
            with act.Fori(2, SLOT_TILES - 2, 2) as s:
                for i in range(2):
                    if i == 0:
                        rt_silu(s + 1, 1)
                        rt_out(s, 0)
                    else:
                        rt_silu(s + 2, 0)
                        rt_out(s + 1, 1)
            rt_out(SLOT_TILES - 1, (SLOT_TILES - 1) % 2)

            ln_exp_tables()

            def fin(q, i):
                act.wait_ge(f_mv, q + 1)
                nc.scalar.activation(fln[i][:], fmv[i][:, :, 1], ACT.Ln, bias=epsc[:])
                nc.scalar.activation(fnm[i][:], fmv[i][:, :, 0], ACT.Identity, scale=-1.0).then_inc(f_rs, 1)
                act.wait_ge(f_rs, 3 * q + 1)
                nc.scalar.activation(frs[i][:], fln[i][:], ACT.Exp, scale=-0.5).then_inc(f_rs, 1)
                act.wait_ge(f_rs, 3 * q + 2)
                for h in range(2):
                    last = nc.scalar.activation(fnm[i][:, h:h + 1], fnm[i][:, h:h + 1], ACT.Identity,
                                                scale=frs[i][:, h:h + 1])
                last.then_inc(f_rs, 1)
                act.wait_ge(f_rs, 3 * q + 3)
                for h in range(2):
                    last = nc.scalar.activation(fy[i][:, h, :], fy[i][:, h, :], ACT.Identity,
                                                scale=frs[i][:, h:h + 1], bias=fnm[i][:, h:h + 1])
                last.then_inc(f_normed, 1)

            with act.Fori(0, NT // 2 - FRING + 1, FRING) as q:
                for i in range(FRING):
                    fin(q + i, i)

        VF_PER = 10
        VB_PER = 2

        @block.vector
        def _(dve):
            nc.vector.memset(epsc[:], EPS)
            nc.vector.memset(mone[:], -1.0)
            for i in range(RING):
                nc.vector.memset(decay[i][:], 0.0)
            dve.wait_ge(consts, 16 * NCONST)
            nc.vector.tensor_copy(w_dt[:], xp[:, :, 0:1].broadcast_to([P, C, P]))
            for g in range(4):
                nc.vector.tensor_copy(w_bc[:, :, g, :], xp[:, :, 1:1 + G3])
            dve.wait_ge(ident_made, 2)
            nc.vector.tensor_tensor(sel_f[:], ident[:, 0:G3], ident[:, 64:64 + G3], ALU.add).then_inc(vf, 1)
            dve.wait_ge(vf, 1)
            nc.vector.tensor_tensor(sel[:], sel_f[:], ident[:, 96:96 + G3], ALU.add)
            dve.wait_ge(aexp, 1)
            nc.vector.tensor_scalar(aneg[:], alog[:], -1.0, None, ALU.mult).then_inc(setup, 1)
            VF0 = 1

            class Chain:

                def __init__(self, s, per, base):
                    self.s, self.per, self.base, self.n = s, per, base, 0

                def link(self, b, ins):
                    self.n += 1
                    ins.then_inc(self.s, 1)
                    dve.wait_ge(self.s, b * self.per + self.base + (self.n - 1) % self.per + 1)

            cf = Chain(vf, VF_PER, VF0)
            cb = Chain(vb, VB_PER, 0)

            def stats(i, chain, b, src):
                for j in range(J):
                    last = nc.vector.bn_stats(out=bst[i][:, j, :], in_=src[:, j, :])
                chain.link(b, last)
                nc.vector.memset(carrier[:], 0.0)
                for j in range(J):
                    last = nc.vector.bn_aggr(out=mv[i][:, j, :], in_=bst[i][:, j, :])
                last.then_inc(mv_ready[i], 1)

            def normed(i, b, dst, src):
                dve.wait_ge(rs_ready[i], 2 * (b + 1))
                dve.wait_ge(mv_ready[i], b + 1)
                for j in range(J):
                    last = nc.vector.tensor_scalar(dst[:, j, :], src[:, j, :], mv[i][:, j, 0:1],
                                                   rstd[i][:, j:j + 1], ALU.subtract, ALU.mult)
                return last

            def front(f, par, slot_):
                first = isinstance(f, int) and f == 0
                if slot_ == 1:
                    dve.wait_ge(x_loaded, 16 * (f + 1))
                    stats(0, cf, f, xin)
                if slot_ == 3:
                    normed(0, f, h0[par], xin).then_inc(h0_ready, 1)
                    dve.wait_ge(h0_ready, f + 1)
                    stats(1, cf, f, h0[par])
                if slot_ in (7, 8):
                    pair = (0, 1) if slot_ == 7 else (2, 3)
                    dve.wait_ge(tap_done, C * f + pair[1] + 1)
                    for s in range(1, TAPS):
                        for c in pair:
                            last = nc.vector.scalar_tensor_tensor(
                                out=acc[:, c, s:L], in0=sq[:, c, 0:L - s],
                                scalar=cw[:, c, TAPS - 1 - s:TAPS - s], in1=acc[:, c, s:L],
                                op0=ALU.mult, op1=ALU.add)
                            if s == TAPS - 1:
                                last.then_inc(conv_done, 1)
                        if s < TAPS - 1:
                            cf.link(f, last)
                if slot_ == 12:
                    dve.wait_ge(proj_ready, f + 1)
                    cf.link(f, nc.vector.tensor_copy(parts[par][:], psG[:]))
                    last = nc.vector.tensor_tensor(rest[64:P], psG[64:P, :], parts[par][64:P], ALU.subtract)
                    cf.link(f, last)
                    nc.vector.tensor_copy(parts[par][64:P], rest[64:P]).then_inc(parts_ready, 1)
                    dve.wait_ge(parts_ready, 2 * f + 1)
                    nc.vector.tensor_tensor(parts[par][96:P], rest[96:P], parts[par][96:P],
                                            ALU.subtract).then_inc(parts_ready, 1)
                if slot_ == 14:
                    dve.wait_ge(loss_ready, f + 1)
                    dve.wait_ge(sq_ready, f + 1)
                    cf.link(f, nc.vector.scalar_tensor_tensor(out=yv[:], in0=yv[:], scalar=LN_MARGIN, in1=sq[:],
                                                              op0=ALU.add, op1=ALU.min))
                    cf.link(f, nc.vector.tensor_tensor(tmp[:], tmp[:], yv[:], ALU.subtract))
                    nc.vector.scalar_tensor_tensor(out=dt[par][:], in0=acc[:], scalar=0.0, in1=tmp[:],
                                                   op0=ALU.max, op1=ALU.add).then_inc(dt_ready, 1)

            def back(b, par, slot_):
                if slot_ == 0:
                    dve.wait_ge(summed, N * (b + 1))
                    for c in range(C):
                        last = nc.vector.scalar_tensor_tensor(out=yv[:, c], in0=xh[par][:, c],
                                                              scalar=dcol[:, c:c + 1], in1=psY[:, c],
                                                              op0=ALU.mult, op1=ALU.add)
                    last.then_inc(yv_done, 1)
                if slot_ == 3:
                    for h in range(2):
                        dve.wait_ge(oproj_ready, 2 * b + h + 1)
                        last = nc.vector.tensor_tensor(ao[:, 2 * h:2 * h + 2].rearrange("p a c -> p (a c)"),
                                                       (psF, psG)[h][:],
                                                       h0[par][:, 2 * h:2 * h + 2].rearrange("p a c -> p (a c)"),
                                                       ALU.add)
                    last.then_inc(ao_done, 1)
                    dve.wait_ge(ao_done, b + 1)
                    stats(2, cb, b, ao)
                if slot_ == 9:
                    dve.wait_ge(xres_loaded, 16 * (b + 1))
                    dve.wait_ge(x1_normed, b + 1)
                    nc.vector.tensor_tensor(x1[:], x1[:], xres[:], ALU.add).then_inc(x1_ready, 1)
                if slot_ == 10:
                    dve.wait_ge(x1_ready, b + 1)
                    stats(3, cb, b, x1)
                if slot_ == 15:
                    dve.wait_ge(logit_ready, b + 1)
                    nc.vector.tensor_copy(logits[:, bass.ds(b * J, J), :].rearrange("p j e -> p (j e)"),
                                          psF[:, 0:J * E]).then_inc(logit_kept, 1)

            def beside(i, par, do_front, do_back, d):
                if do_back:
                    back(i - 1, 1 - par, d)
                if do_front:
                    front(i + 1, 1 - par, d)

            def iteration(i, par, do_front, do_back):
                for d in range(N):
                    n = i * N + d
                    dve.wait_ge(decay_ready, n + 1)
                    dve.wait_ge(bx_ready, n + 1)
                    w = st[d % RING]
                    nc.vector.tensor_tensor_scan(w[:].rearrange("p c t -> p (c t)"),
                                                 decay[d % RING][:].rearrange("p c t -> p (c t)"),
                                                 w[:].rearrange("p c t -> p (c t)"),
                                                 0.0, ALU.mult, ALU.add).then_inc(scanned, 1)
                    late = d in (0, 3)
                    if not late:
                        beside(i, par, do_front, do_back, d)
                    dve.wait_ge(c_bcast, n + 1)
                    dve.wait_ge(scanned, n + 1)
                    nc.vector.tensor_tensor(w[:], w[:],
                                            psC[:].unsqueeze(1).broadcast_to([P, C, L]),
                                            ALU.mult).then_inc(weighted, 1)
                    if late:
                        beside(i, par, do_front, do_back, d)

            for s in range(N):
                front(0, 0, s)
            iteration(0, 0, True, False)
            with dve.Fori(1, NB - 2, 2) as i:
                iteration(i, 1, True, True)
                iteration(i + 1, 0, True, True)
            iteration(NB - 1, 1, False, True)
            for s in range(N):
                back(NB - 1, 1, s)

            rn = [0]

            def link(ins):
                rn[0] += 1
                ins.then_inc(rc, 1)
                dve.wait_ge(rc, rn[0])

            def bt(a):
                return a.unsqueeze(2).broadcast_to([P, NT, E])

            def be(a):
                return a.unsqueeze(1).broadcast_to([P, NT, E])

            oh, cnt, incl, q = rt["oh"], rt["cnt"], rt["incl"], rt["q"]
            dve.wait_ge(iotas, 2)
            dve.wait_ge(logit_kept, NB)
            nc.vector.tensor_copy(iotaJ[:], iotaJi[:])
            link(nc.vector.tensor_copy(iotaE[:], iotaEi[:]))
            nc.vector.tensor_reduce(out=mx[:], in_=logits[:], axis=AX.X, op=ALU.max).then_inc(mx_ready, 1)
            dve.wait_ge(mx_ready, 1)
            link(nc.vector.tensor_tensor(q[:], logits[:], bt(mx[:]), ALU.is_equal))
            link(nc.vector.tensor_tensor(q[:], q[:], be(iotaE[:]), ALU.mult))
            link(nc.vector.tensor_reduce(out=mn[:], in_=q[:], axis=AX.X, op=ALU.min))
            nc.vector.tensor_tensor(oh[:], be(iotaE[:]), bt(mn[:]), ALU.is_equal).then_inc(oh_ready, 1)
            def sh_act(g, gp, c):
                u = g * FC + c
                dve.wait_ge(s_silu, u + 1)
                if c == 0 and not (isinstance(g, int) and g < 2):
                    dve.wait_ge(s_down, 2 * (g - 1))
                nc.vector.tensor_tensor(actS[gp][:, c], sg[c % 2][:], psY[:, 2 + c % 2], ALU.mult).then_inc(s_act, 1)

            sh_act(0, 0, 0)
            sh_act(0, 0, 1)
            dve.wait_ge(rank_ready, 2)
            link(nc.vector.tensor_copy(cnt[:].rearrange("p t e -> p (t e)"), psC[:, 0:NT * E]))
            for e in range(E):
                last = nc.vector.tensor_tensor_scan(incl[:, :, e], onesT[:], cnt[:, :, e], 0.0, ALU.mult, ALU.add)
            link(last)
            link(nc.vector.tensor_tensor(q[:].rearrange("p t e -> p (t e)"), psB[:, 0:NT * E],
                                         incl[:].rearrange("p t e -> p (t e)"), ALU.add))
            link(nc.vector.tensor_tensor(q[:], q[:], cnt[:], ALU.subtract))
            link(nc.vector.tensor_scalar(ti[:], incl[:, NT - 1, :], float(P - 1), None, ALU.add))
            link(nc.vector.tensor_scalar(ti[:], ti[:], 7, None, ALU.arith_shift_right))
            link(nc.vector.tensor_copy(tf[:], ti[:]))
            link(nc.vector.tensor_tensor_scan(tend[:], onesT[:, 0:E], tf[:], 0.0, ALU.mult, ALU.add))
            link(nc.vector.tensor_tensor(tstart[:], tend[:], tf[:], ALU.subtract))
            link(nc.vector.tensor_scalar(tstart[:], tstart[:], float(P), None, ALU.mult))
            link(nc.vector.tensor_tensor(q[:], q[:], be(tstart[:]), ALU.add))
            link(nc.vector.tensor_tensor(q[:], q[:], oh[:], ALU.mult))
            link(nc.vector.tensor_reduce(out=slotf[:], in_=q[:], axis=AX.X, op=ALU.add))
            nc.vector.tensor_copy(slot[:], slotf[:]).then_inc(slot_ready, 1)
            link(nc.vector.tensor_tensor(le[:], tend[0:1, :].unsqueeze(1).broadcast_to([1, SLOT_TILES, E]),
                                         iotaJ[:].unsqueeze(2).broadcast_to([1, SLOT_TILES, E]), ALU.is_le))
            link(nc.vector.tensor_reduce(out=exf[:], in_=le[:], axis=AX.X, op=ALU.add))
            nc.vector.tensor_scalar(exi[:], exf[:], float(E - 1), None, ALU.min).then_inc(ex_ready, 1)

            for u in range(2, 2 * FC):
                sh_act(u // FC, u // FC, u % FC)
            with dve.Fori(2, NB - 1, 2) as g:
                for h in range(2):
                    for c in range(FC):
                        sh_act(g + h, h, c)

            def copy_xsT(s, i):
                dve.wait_ge(xsT_ready, s + 1)
                if not (isinstance(s, int) and s < 2):
                    dve.wait_ge(r_up, s - 1)
                nc.vector.tensor_copy(xsT[i][:].rearrange("p k t -> p (k t)"), psB[:, 0:KC * P]).then_inc(xsT_copied, 1)

            def rt_act(s, i):
                dve.wait_ge(r_silu, s + 1)
                if not (isinstance(s, int) and s < 2):
                    dve.wait_ge(actT_ready, s - 1)
                nc.vector.tensor_tensor(actN[i][:], sg[i][:], psY[:, 2 + i], ALU.mult).then_inc(r_act, 1)

            def copy_actT(s, i):
                dve.wait_ge(actT_ready, s + 1)
                if not (isinstance(s, int) and s < 2):
                    dve.wait_ge(r_down, s - 1)
                nc.vector.tensor_copy(actT[i][:].rearrange("p k t -> p (k t)"), psC[:]).then_inc(actT_copied, 1)

            S = SLOT_TILES
            dve.wait_ge(s_down, 2 * NB)
            copy_xsT(0, 0)
            copy_xsT(1, 1)
            rt_act(0, 0)
            for s in (0, 1):
                copy_xsT(s + 2, s % 2)
                copy_actT(s, s % 2)
                rt_act(s + 1, (s + 1) % 2)
            with dve.Fori(2, S - 4, 2) as s:
                for i in range(2):
                    copy_xsT(s + i + 2, i)
                    copy_actT(s + i, i)
                    rt_act(s + i + 1, 1 - i)
            for s in range(S - 3, S):
                if s + 2 < S:
                    copy_xsT(s + 2, s % 2)
                copy_actT(s, s % 2)
                if s + 1 < S:
                    rt_act(s + 1, (s + 1) % 2)

            def fin_sum(q, i):
                dve.wait_ge(gathered[i], (32 // FRING) * (q - i) + 32)
                nc.vector.tensor_tensor(fy[i][:], fy[i][:], ysh[:, bass.ds(2 * q, 2), :], ALU.add).then_inc(f_chain, 1)
                dve.wait_ge(f_chain, 2 * q + 1)
                for h in range(2):
                    last = nc.vector.bn_stats(out=fst[i][:, h, :], in_=fy[i][:, h, :])
                last.then_inc(f_chain, 1)
                dve.wait_ge(f_chain, 2 * q + 2)
                nc.vector.memset(carrier[:], 0.0)
                for h in range(2):
                    last = nc.vector.bn_aggr(out=fmv[i][:, h, :], in_=fst[i][:, h, :])
                last.then_inc(f_mv, 1)

            def fin_out(q, i, dst, first):
                dve.wait_ge(f_normed, q + 1)
                pair = dst[:, bass.ds(2 * (q - first), 2), :]
                nc.vector.tensor_tensor(pair, fy[i][:], pair, ALU.add).then_inc(f_ready, 1)

            NQ = NT // 2
            LAG = 2
            for q in range(LAG):
                fin_sum(q, q)
            dve.wait_ge(f_loaded[0], 16 * (NB // 2))
            for q in range(NQ):
                if q == NQ // 2:
                    dve.wait_ge(f_loaded[1], 16 * (NB // 2))
                if q + LAG < NQ:
                    fin_sum(q + LAG, (q + LAG) % FRING)
                fin_out(q, q % FRING, (fx0, fx1)[q // (NQ // 2)], q // (NQ // 2) * (NQ // 2))

        @block.tensor
        def _(pe):
            pe.wait_ge(ident_made, 2)
            pe.wait_ge(consts, 16 * NCONST)
            pe.wait_ge(setup, 1)

            def bcast_row(dst, par, r):
                return nc.tensor.matmul(dst[:], sel[:, r:r + 1].broadcast_to([P, P]), parts[par][:],
                                        start=True, stop=True)

            def front(f, par, slot_):
                first = isinstance(f, int) and f == 0
                if slot_ == 4:
                    pe.wait_ge(h1_ready, f + 1)
                    if not first:
                        pe.wait_ge(z_done, f)
                        pe.wait_ge(parts_ready, 2 * f)
                    if not (isinstance(f, int) and f < 2):
                        pe.wait_ge(ao_done, f - 1)
                    for k in range(KC):
                        for j in range(J):
                            last = nc.tensor.transpose((psF, psG)[k][:, j * P:(j + 1) * P],
                                                       h1[:, j, k * P:(k + 1) * P], ident[:])
                        last.then_inc(h1T_ready, 1)
                if slot_ in (5, 6):
                    pe.wait_ge(hT_ready, f + 1)
                    for c in (0, 1) if slot_ == 5 else (2, 3):
                        if c >= 2:
                            pe.wait_ge(tap_done, C * f + c - 1)
                        for k in range(KC):
                            last = nc.tensor.matmul((psF, psG)[c % 2][:], win[:, k, c * P:(c + 1) * P], hT[:, k],
                                                    start=(k == 0), stop=(k == KC - 1))
                        last.then_inc(inproj_ready, 1)
                if slot_ == 9:
                    pe.wait_ge(xh_ready, f + 1)
                    for c in range(C):
                        last = nc.tensor.matmul(psF[:], w_dt[:, c], xh[par][:, c], start=(c == 0), stop=(c == C - 1))
                    last.then_inc(dtin_ready, 1)
                if slot_ == 10:
                    for c in range(C):
                        last = nc.tensor.matmul(psG[:], w_bc[:, c].rearrange("p g r -> p (g r)"), xh[par][:, c],
                                                start=(c == 0), stop=(c == C - 1))
                    last.then_inc(proj_ready, 1)

            def back(b, slot_, fronts):
                if slot_ in (1, 2):
                    pe.wait_ge(ys_ready, b + 1)
                    pe.wait_ge(z_done, fronts)
                    pe.wait_ge(parts_ready, 2 * fronts)
                    h = slot_ - 1
                    for j in (2 * h, 2 * h + 1):
                        for c in range(C):
                            last = nc.tensor.matmul((psF, psG)[h][:, (j % 2) * DIM:(j % 2 + 1) * DIM],
                                                    yv[:, c, j * P:(j + 1) * P], wout[:, c],
                                                    start=(c == 0), stop=(c == C - 1))
                    last.then_inc(oproj_ready, 1)
                if slot_ == 13:
                    pe.wait_ge(xn_ready, b + 1)
                    if isinstance(fronts, int) and fronts == NB:
                        pe.wait_ge(ao_done, b + 1)
                    else:
                        pe.wait_ge(z_done, fronts + 1)
                        pe.wait_ge(parts_ready, 2 * (fronts + 1))
                    for k in range(KC):
                        for j in range(J):
                            last = nc.tensor.transpose((psF, psG)[k][:, j * P:(j + 1) * P],
                                                       xn[:, j, k * P:(k + 1) * P], ident[:])
                        last.then_inc(xnT_ready, 1)
                if slot_ == 14:
                    pe.wait_ge(xnT_copied, b + 1)
                    for j in range(J):
                        for k in range(KC):
                            last = nc.tensor.matmul(psF[:, j * E:(j + 1) * E], xnTb[:, k, j * P:(j + 1) * P],
                                                    gw[:, k], start=(k == 0), stop=(k == KC - 1))
                    last.then_inc(logit_ready, 1)
                if slot_ == 15:
                    pe.wait_ge(logit_kept, b + 1)

            def iteration(i, par, do_front, do_back, last):
                for d in range(N):
                    n = i * N + d
                    pe.wait_ge(weighted, n + 1)
                    if not (last and d == N - 1):
                        bcast_row(psC, par if d < N - 1 else 1 - par, N + (d + 1) % N).then_inc(c_bcast, 1)
                    if not (last and d >= N - 3):
                        if d == N - 3:
                            pe.wait_ge(parts_ready, 2 * (i + 2))
                        pe.wait_ge(b_copied, n + 3)
                        bcast_row(psB, par if d < N - 3 else 1 - par, (d + 3) % N).then_inc(b_bcast, 1)
                    if do_back:
                        back(i - 1, d, i + 1)
                    if do_front:
                        front(i + 1, 1 - par, d)
                    if d == 0 and do_back:
                        pe.wait_ge(yv_done, i)
                    for c in range(C):
                        s = nc.tensor.matmul(psY[:, c], ident[:], st[d % RING][:, c], start=(d == 0), stop=(d == N - 1))
                    s.then_inc(summed, 1)

            for s in range(N):
                front(0, 0, s)
            pe.wait_ge(parts_ready, 2)
            bcast_row(psC, 0, N).then_inc(c_bcast, 1)
            for r in range(3):
                if r > 0:
                    pe.wait_ge(b_copied, r)
                bcast_row(psB, 0, r).then_inc(b_bcast, 1)
            iteration(0, 0, True, False, False)
            with pe.Fori(1, NB - 2, 2) as i:
                iteration(i, 1, True, True, False)
                iteration(i + 1, 0, True, True, False)
            iteration(NB - 1, 1, False, True, True)
            for s in range(N):
                back(NB - 1, s, NB)

            def sh_up_(g, c, i):
                u = g * FC + c
                if c == 0:
                    pe.wait_ge(xg_loaded[i], 8 * (g - i) + 16)
                if not (isinstance(u, int) and u < 2):
                    pe.wait_ge(s_act, u - 1)
                for w, bank in ((shg, psY[:, c % 2]), (shu, psY[:, 2 + c % 2])):
                    for k in range(KC):
                        last = nc.tensor.matmul(bank, w[:, k, c * P:(c + 1) * P], xg[i][:, k],
                                                start=(k == 0), stop=(k == KC - 1))
                last.then_inc(s_up, 1)

            pe.wait_ge(yv_done, NB)
            pe.wait_ge(sh_loaded, 48)
            sh_up_(0, 0, 0)
            sh_up_(0, 1, 0)

            pe.wait_ge(oh_ready, 1)
            oh = rt["oh"][:].rearrange("p t e -> p (t e)")
            nc.tensor.matmul(psB[:, 0:NT * E], upper[:], oh, start=True, stop=True).then_inc(rank_ready, 1)
            nc.tensor.matmul(psC[:, 0:NT * E], ones[:], oh, start=True, stop=True).then_inc(rank_ready, 1)

            def sh_down_(g, gp):
                pe.wait_ge(s_act, (g + 1) * FC)
                for j in range(J):
                    if j % 2 == 0 and not (isinstance(g, int) and g == 0):
                        pe.wait_ge(s_kept, 2 * g + j // 2 - 1)
                    for c in range(FC):
                        last = nc.tensor.matmul((psF, psG)[j // 2][:, (j % 2) * DIM:(j % 2 + 1) * DIM],
                                                actS[gp][:, c, j * P:(j + 1) * P], shd[:, c],
                                                start=(c == 0), stop=(c == FC - 1))
                    if j % 2:
                        last.then_inc(s_down, 1)

            for u in range(2, 2 * FC):
                sh_up_(u // FC, u % FC, u // FC)
            sh_down_(0, 0)
            with pe.Fori(2, NB - 1, 2) as g:
                for h in range(2):
                    for c in range(FC):
                        sh_up_(g + h, c, h)
                    sh_down_(g + h - 1, 1 - h)
            sh_down_(NB - 1, 1)

            def xsT_(s, i):
                pe.wait_ge(xsl_loaded[i], 8 * (s - i) + 16)
                if not (isinstance(s, int) and s == 0):
                    pe.wait_ge(xsT_copied, s)
                for k in range(KC):
                    last = nc.tensor.transpose(psB[:, k * P:(k + 1) * P], xsl[i][:, k * P:(k + 1) * P], ident[:])
                last.then_inc(xsT_ready, 1)

            def up_(s, i):
                pe.wait_ge(xsT_copied, s + 1)
                if not (isinstance(s, int) and s < 2):
                    pe.wait_ge(r_act, s - 1)
                for w, bank in ((wg, psY[:, i]), (wu, psY[:, 2 + i])):
                    for k in range(KC):
                        last = nc.tensor.matmul(bank, xsT[i][:, k], w[:, bass.ds(ereg[i], 1), k].rearrange("p a n -> p (a n)"),
                                                start=(k == 0), stop=(k == KC - 1))
                last.then_inc(r_up, 1)

            def actT_(s, i):
                pe.wait_ge(r_act, s + 1)
                if not (isinstance(s, int) and s == 0):
                    pe.wait_ge(actT_copied, s)
                for c in range(FC):
                    last = nc.tensor.transpose(psC[:, c * P:(c + 1) * P], actN[i][:, c * P:(c + 1) * P], ident[:])
                last.then_inc(actT_ready, 1)

            def down_(s, i):
                pe.wait_ge(actT_copied, s + 1)
                if not (isinstance(s, int) and s < 2):
                    pe.wait_ge(yo_ready, s - 1)
                for c in range(FC):
                    last = nc.tensor.matmul((psF, psG)[i][:, 0:DIM], actT[i][:, c],
                                            wd[:, bass.ds(ereg[i], 1), c].rearrange("p a n -> p (a n)"),
                                            start=(c == 0), stop=(c == FC - 1))
                last.then_inc(r_down, 1)

            S = SLOT_TILES
            ereg = [None, None]

            def expert(s, i):
                ereg[i] = pe.value_load(exi[0:1, bass.ds(s, 1)], min_val=0, max_val=E - 1)

            pe.wait_ge(ex_ready, 1)
            pe.wait_ge(rt_loaded, 16 * 3 * E)
            xsT_(0, 0)
            xsT_(1, 1)
            expert(0, 0)
            up_(0, 0)
            pe.wait_ge(s_kept, 2 * NB)

            def step(s, i, ahead, more):
                if ahead:
                    xsT_(s + 2, i)
                actT_(s, i)
                if more:
                    expert(s + 1, 1 - i)
                    up_(s + 1, 1 - i)
                expert(s, i)
                down_(s, i)

            step(0, 0, True, True)
            step(1, 1, True, True)
            with pe.Fori(2, S - 4, 2) as s:
                step(s, 0, True, True)
                step(s + 1, 1, True, True)
            for s in range(S - 3, S):
                step(s, s % 2, s + 2 < S, s + 1 < S)


def kernel(**inputs):
    import concourse.bacc as _bacc
    from concourse.bass_utils import run_bass_kernel_spmd as _run

    def given(name, transposed=False):
        a = np.asarray(inputs[name])
        return np.ascontiguousarray(a.T if transposed else a)

    def columns(name):
        return np.ascontiguousarray(np.asarray(inputs[name]).reshape(-1, P).T)

    data = {
        "x": given("L0_attn_x"),
        "winT": given("L0_attn_in_proj_w", True),
        "conv_w": given("L0_attn_conv_w"),
        "xprojT": given("L0_attn_x_proj_w", True),
        "dt_w": columns("L0_attn_dt_proj_w"),
        "dt_b": columns("L0_attn_dt_proj_b"),
        "A_log": given("L0_attn_A_log"),
        "D": columns("L0_attn_D"),
        "woutT": given("L0_attn_out_proj_w", True),
        "norm_w": columns("L0_attn_norm_w"),
        "norm_b": columns("L0_attn_norm_b"),
        "gate_w": given("L0_ffn_gate_w"),
        "sh_gate": given("L0_ffn_sh_gate"),
        "sh_up": given("L0_ffn_sh_up"),
        "sh_down": given("L0_ffn_sh_down"),
        "rt_gate": given("L0_ffn_rt_gate"),
        "rt_up": given("L0_ffn_rt_up"),
        "rt_down": given("L0_ffn_rt_down"),
    }
    nc = _bacc.Bacc("TRN2", target_bir_lowering=False, num_devices=1)
    args = [nc.dram_tensor(f"in_{n}", a.shape, mybir.dt.from_np(a.dtype), kind="ExternalInput").ap()
            for n, a in data.items()]
    res = nc.dram_tensor("result", data["x"].shape, F32, kind="ExternalOutput").ap()
    build(nc, *args, res)
    r = _run(nc, [{f"in_{n}": a for n, a in data.items()}], core_ids=[0])
    return r.results[0]["result"]
```
